# Optimizing a Trainium2 kernel written in Bass

```python
import numpy as np
import jax
import jax.numpy as jnp

def _softmax(x, axis=-1):
    return jax.nn.softmax(x, axis=axis)

def _gelu(x):
    return jax.nn.gelu(x, approximate=True)

def _silu(x):
    return jax.nn.silu(x)

def _sigmoid(x):
    return jax.nn.sigmoid(x)

def _layernorm(x, axis=-1, eps=1e-05):
    m = jnp.mean(x, axis=axis, keepdims=True)
    v = jnp.var(x, axis=axis, keepdims=True)
    return (x - m) / jnp.sqrt(v + eps)

def _scatter_add(tgt, idx, src, axis=0):
    return tgt.at[idx].add(src)

def _segment_sum(src, seg, n):
    return jax.ops.segment_sum(src, seg, n)
kernel_name = 'mk_seq_preln_d2_jaxref_r8_2a11ef'

def setup_inputs(seed: int=0):
    np.random.seed(seed)
    _w = jnp.asarray

    def _L0_attn_setup():
        import math
        import jax, jax.numpy as jnp
        import numpy as np
        NUM_HEAD = 16

        def get_slopes(n):

            def pow2(n):
                start = 2 ** (-2 ** (-(math.log2(n) - 3)))
                return [start * start ** i for i in range(n)]
            if math.log2(n).is_integer():
                return pow2(n)
            c = 2 ** math.floor(math.log2(n))
            return pow2(c) + get_slopes(2 * c)[0::2][:n - c]
        key = jax.random.key(seed)
        ks = jax.random.split(key, 9)
        B, T, C = (2, 256, 256)
        x = jax.random.normal(ks[0], (B, T, C), dtype=jnp.float32)
        std = 0.02
        Wq = std * jax.random.normal(ks[1], (C, C), dtype=jnp.float32)
        Wk = std * jax.random.normal(ks[2], (C, C), dtype=jnp.float32)
        Wv = std * jax.random.normal(ks[3], (C, C), dtype=jnp.float32)
        Wo = 0.02 / np.sqrt(2 * 24) * jax.random.normal(ks[4], (C, C), dtype=jnp.float32)
        bq = jnp.zeros((C,), jnp.float32)
        bk = jnp.zeros((C,), jnp.float32)
        bv = jnp.zeros((C,), jnp.float32)
        bo = jnp.zeros((C,), jnp.float32)
        return {'x': x, 'Wq': Wq, 'bq': bq, 'Wk': Wk, 'bk': bk, 'Wv': Wv, 'bv': bv, 'Wo': Wo, 'bo': bo}
    _L0_attn_in = _L0_attn_setup()

    def _L0_ffn_setup():
        import jax, jax.numpy as jnp
        import numpy as np
        DIM = 256
        HID = 704
        ZERO_POINT = 128.0

        def _qlinear(x, wq, scale):
            W = (wq.astype(jnp.float32) - ZERO_POINT) * scale[:, None]
            return jnp.einsum('bsd,hd->bsh', x, W)
        key = jax.random.key(seed)
        ks = jax.random.split(key, 7)
        B, S = (4, 256)
        sg = jax.random.uniform(ks[1], (HID,)) * (0.02 / np.sqrt(DIM)) + 0.0001
        su = jax.random.uniform(ks[3], (HID,)) * (0.02 / np.sqrt(DIM)) + 0.0001
        sd = jax.random.uniform(ks[5], (DIM,)) * (0.02 / np.sqrt(HID)) + 0.0001
        return {'x': jax.random.normal(ks[0], (B, S, DIM), dtype=jnp.float32), 'wq_gate': jax.random.randint(ks[2], (HID, DIM), 0, 32, dtype=jnp.int32), 's_gate': sg, 'wq_up': jax.random.randint(ks[4], (HID, DIM), 0, 32, dtype=jnp.int32), 's_up': su, 'wq_down': jax.random.randint(ks[6], (DIM, HID), 0, 32, dtype=jnp.int32), 's_down': sd}
    _L0_ffn_in = _L0_ffn_setup()

    def _L1_attn_setup():
        import jax, jax.numpy as jnp
        import numpy as np
        NH = 16
        key = jax.random.key(seed)
        ks = jax.random.split(key, 5)
        B, T, D = (2, 256, 256)
        scale = 0.02
        return {'x': jax.random.normal(ks[0], (B, T, D), dtype=jnp.float32), 'Wq': jax.random.normal(ks[1], (D, D), dtype=jnp.float32) * scale, 'Wk': jax.random.normal(ks[2], (D, D), dtype=jnp.float32) * scale, 'Wv': jax.random.normal(ks[3], (D, D), dtype=jnp.float32) * scale, 'Wo': jax.random.normal(ks[4], (D, D), dtype=jnp.float32) * scale}
    _L1_attn_in = _L1_attn_setup()

    def _L1_ffn_setup():
        import jax, jax.numpy as jnp
        import numpy as np
        B, S, H, I = (1, 64, 256, 768)

        def _quantized_matmul(x, w, scale):
            wq = w.astype(jnp.float8_e4m3fn).astype(x.dtype)
            y = jnp.einsum('bsi,io->bso', x, wq)
            return y * scale
        key = jax.random.key(seed)
        ks = jax.random.split(key, 7)
        return {'x': jax.random.normal(ks[0], (B, S, H), dtype=jnp.float32), 'gate_w': jax.random.normal(ks[1], (H, I), dtype=jnp.float32) * 0.02, 'up_w': jax.random.normal(ks[2], (H, I), dtype=jnp.float32) * 0.02, 'down_w': jax.random.normal(ks[3], (I, H), dtype=jnp.float32) * 0.02, 'gate_scale': jax.random.uniform(ks[4], (I,), dtype=jnp.float32, minval=0.5, maxval=1.5), 'up_scale': jax.random.uniform(ks[5], (I,), dtype=jnp.float32, minval=0.5, maxval=1.5), 'down_scale': jax.random.uniform(ks[6], (H,), dtype=jnp.float32, minval=0.5, maxval=1.5)}
    _L1_ffn_in = _L1_ffn_setup()
    _d = {'L0_attn_x': _L0_attn_in['x'], 'L0_attn_Wq': _L0_attn_in['Wq'], 'L0_attn_bq': _L0_attn_in['bq'], 'L0_attn_Wk': _L0_attn_in['Wk'], 'L0_attn_bk': _L0_attn_in['bk'], 'L0_attn_Wv': _L0_attn_in['Wv'], 'L0_attn_bv': _L0_attn_in['bv'], 'L0_attn_Wo': _L0_attn_in['Wo'], 'L0_attn_bo': _L0_attn_in['bo'], 'L0_ffn_wq_gate': _L0_ffn_in['wq_gate'], 'L0_ffn_s_gate': _L0_ffn_in['s_gate'], 'L0_ffn_wq_up': _L0_ffn_in['wq_up'], 'L0_ffn_s_up': _L0_ffn_in['s_up'], 'L0_ffn_wq_down': _L0_ffn_in['wq_down'], 'L0_ffn_s_down': _L0_ffn_in['s_down'], 'L1_attn_Wq': _L1_attn_in['Wq'], 'L1_attn_Wk': _L1_attn_in['Wk'], 'L1_attn_Wv': _L1_attn_in['Wv'], 'L1_attn_Wo': _L1_attn_in['Wo'], 'L1_ffn_gate_w': _L1_ffn_in['gate_w'], 'L1_ffn_up_w': _L1_ffn_in['up_w'], 'L1_ffn_down_w': _L1_ffn_in['down_w'], 'L1_ffn_gate_scale': _L1_ffn_in['gate_scale'], 'L1_ffn_up_scale': _L1_ffn_in['up_scale'], 'L1_ffn_down_scale': _L1_ffn_in['down_scale']}
    _x0 = _d['L0_attn_x']
    _d['L0_attn_x'] = jax.random.normal(jax.random.fold_in(jax.random.key(seed), 1), (1, 1024, 256), dtype=_x0.dtype)
    del _x0
    return _d

def reference(L0_attn_x, L0_attn_Wq, L0_attn_bq, L0_attn_Wk, L0_attn_bk, L0_attn_Wv, L0_attn_bv, L0_attn_Wo, L0_attn_bo, L0_ffn_wq_gate, L0_ffn_s_gate, L0_ffn_wq_up, L0_ffn_s_up, L0_ffn_wq_down, L0_ffn_s_down, L1_attn_Wq, L1_attn_Wk, L1_attn_Wv, L1_attn_Wo, L1_ffn_gate_w, L1_ffn_up_w, L1_ffn_down_w, L1_ffn_gate_scale, L1_ffn_up_scale, L1_ffn_down_scale):

    def _L0_attn_ref(x, Wq, bq, Wk, bk, Wv, bv, Wo, bo):
        import math
        import jax, jax.numpy as jnp
        import numpy as np
        NUM_HEAD = 16

        def get_slopes(n):

            def pow2(n):
                start = 2 ** (-2 ** (-(math.log2(n) - 3)))
                return [start * start ** i for i in range(n)]
            if math.log2(n).is_integer():
                return pow2(n)
            c = 2 ** math.floor(math.log2(n))
            return pow2(c) + get_slopes(2 * c)[0::2][:n - c]
        B, T, C = x.shape
        H = NUM_HEAD
        D = C // H
        slopes = jnp.asarray(get_slopes(H), dtype=jnp.float32)

        def split_heads(y):
            return y.reshape(B, T, H, D).transpose(0, 2, 1, 3)
        q = split_heads(x @ Wq + bq)
        k = split_heads(x @ Wk + bk)
        v = split_heads(x @ Wv + bv)
        attn = jnp.einsum('bhqd,bhkd->bhqk', q, k) / jnp.sqrt(jnp.float32(D))
        alibi = slopes[:, None, None] * (jnp.arange(T, dtype=jnp.float32) - (T - 1))[None, None, :]
        attn = attn + alibi
        causal = jnp.tril(jnp.ones((T, T), dtype=bool))[None, None]
        attn = jnp.where(causal, attn, jnp.finfo(jnp.float32).min)
        p = jax.nn.softmax(attn, axis=-1)
        o = jnp.einsum('bhqk,bhkd->bhqd', p, v).transpose(0, 2, 1, 3).reshape(B, T, C)
        return o @ Wo + bo

    def _L0_ffn_ref(x, wq_gate, s_gate, wq_up, s_up, wq_down, s_down):
        import jax, jax.numpy as jnp
        import numpy as np
        DIM = 256
        HID = 704
        ZERO_POINT = 128.0

        def _qlinear(x, wq, scale):
            W = (wq.astype(jnp.float32) - ZERO_POINT) * scale[:, None]
            return jnp.einsum('bsd,hd->bsh', x, W)
        gate = _qlinear(x, wq_gate, s_gate)
        gate = jax.nn.silu(gate)
        up = _qlinear(x, wq_up, s_up)
        return _qlinear(gate * up, wq_down, s_down)

    def _L1_attn_ref(x, Wq, Wk, Wv, Wo):
        import jax, jax.numpy as jnp
        import numpy as np
        NH = 16
        B, T, D = x.shape
        hd = D // NH
        q = (x @ Wq.T).reshape(B, T, NH, hd).transpose(0, 2, 1, 3)
        k = (x @ Wk.T).reshape(B, T, NH, hd).transpose(0, 2, 1, 3)
        v = (x @ Wv.T).reshape(B, T, NH, hd).transpose(0, 2, 1, 3)
        att = jnp.einsum('bhtd,bhsd->bhts', q, k) / jnp.sqrt(jnp.asarray(hd, x.dtype))
        neg = jnp.finfo(att.dtype).min
        mask = jnp.triu(jnp.full((T, T), neg, dtype=att.dtype), k=1)
        att = att + mask
        w = jax.nn.softmax(att, axis=-1)
        z = jnp.einsum('bhts,bhsd->bhtd', w, v)
        z = z.transpose(0, 2, 1, 3).reshape(B, T, D)
        return z @ Wo.T

    def _L1_ffn_ref(x, gate_w, up_w, down_w, gate_scale, up_scale, down_scale):
        import jax, jax.numpy as jnp
        import numpy as np
        B, S, H, I = (1, 64, 256, 768)

        def _quantized_matmul(x, w, scale):
            wq = w.astype(jnp.float8_e4m3fn).astype(x.dtype)
            y = jnp.einsum('bsi,io->bso', x, wq)
            return y * scale
        gate = jax.nn.silu(_quantized_matmul(x, gate_w, gate_scale))
        up = _quantized_matmul(x, up_w, up_scale)
        fuse = gate * up
        return _quantized_matmul(fuse, down_w, down_scale)
    x = L0_attn_x
    x = x + _L0_attn_ref(_layernorm(x, axis=-1), L0_attn_Wq, L0_attn_bq, L0_attn_Wk, L0_attn_bk, L0_attn_Wv, L0_attn_bv, L0_attn_Wo, L0_attn_bo)
    x = x + _L0_ffn_ref(_layernorm(x, axis=-1), L0_ffn_wq_gate, L0_ffn_s_gate, L0_ffn_wq_up, L0_ffn_s_up, L0_ffn_wq_down, L0_ffn_s_down)
    x = x + _L1_attn_ref(_layernorm(x, axis=-1), L1_attn_Wq, L1_attn_Wk, L1_attn_Wv, L1_attn_Wo)
    x = x + _L1_ffn_ref(_layernorm(x, axis=-1), L1_ffn_gate_w, L1_ffn_up_w, L1_ffn_down_w, L1_ffn_gate_scale, L1_ffn_up_scale, L1_ffn_down_scale)
    return x

_drawn_inputs = setup_inputs


def setup_inputs(seed=0):
    import zlib

    import numpy as np

    out = dict(_drawn_inputs(seed))
    spreads = {'L0_attn_bq': (0.0, 0.8),
     'L0_attn_bk': (0.0, 0.8),
     'L0_attn_bv': (0.0, 0.8),
     'L0_attn_bo': (0.0, 0.1)}
    factors = {'L0_attn_Wq': 8.0,
     'L0_attn_Wk': 8.0,
     'L0_attn_Wv': 8.0,
     'L0_attn_Wo': 8.0,
     'L0_ffn_s_gate': 8.0,
     'L0_ffn_s_up': 8.0,
     'L0_ffn_s_down': 8.0,
     'L1_attn_Wq': 8.0,
     'L1_attn_Wk': 8.0,
     'L1_attn_Wv': 4.018,
     'L1_attn_Wo': 4.317,
     'L1_ffn_gate_scale': 5.343,
     'L1_ffn_up_scale': 6.178,
     'L1_ffn_down_scale': 5.998}
    for name, (base, spread) in spreads.items():
        noise = np.random.default_rng([zlib.crc32(name.encode()), seed]).standard_normal(out[name].shape)
        drawn = base * np.exp(spread * noise) if base else spread * noise
        out[name] = jnp.asarray(drawn.astype(out[name].dtype))
    for name, factor in factors.items():
        out[name] = (out[name] * factor).astype(out[name].dtype)
    return out
```

```python
from contextlib import ExitStack

import numpy as np

import concourse.bass as bass
from concourse import mybir

P = 128
T, C = 1024, 256
NH, HD = 16, 16
HID0, HID1 = 704, 768
NT = T // P
CH = 512
NC = T // CH
CJ = C // P
G = 4
NG = NH // G
TPC = CH // P
LAYERS = 2
HT = 6
NEG = -3.0e38
EPS = 1e-5
ZERO_POINT = 128.0
SCALE = float(HD) ** -0.5

F32, BF16, FP16, I32 = mybir.dt.float32, mybir.dt.bfloat16, mybir.dt.float16, mybir.dt.int32
ALU = mybir.AluOpType
ACT = mybir.ActivationFunctionType
AX_X = mybir.AxisListType.X

Q_PARTS = (0, 0, 0, 1, 1, 2)
K_PARTS = (0, 1, 2, 0, 1, 0)
QK_ROWS = len(Q_PARTS) * HD
ALIBI_ROWS = (3, 0)
MAX_ROWS = 2
K_MAX = [QK_ROWS + a for a in ALIBI_ROWS]
K_EXP = [k + MAX_ROWS for k in K_MAX]


def hid_rows(layer, ht):
    return min(P, (HID0, HID1)[layer] - ht * P)



def ring_a_jobs():
    jobs = []
    for L in range(LAYERS):
        jobs += [("xnT", L, t) for t in range(NT)]
        if L == 0:
            jobs += [("w1T", m) for m in range(4)]
            jobs += [(w, k) for w in ("gateT", "upT", "downT") for k in range(HT // 2)]
        jobs += [("onT", L, t) for t in range(NT)]
        if L == 0:
            jobs += [("ffnT", L, t) for t in range(NT)]
        jobs += [("gate", L, c, ht) for c in range(NC) for ht in range(HT)]
    return jobs


def ring_b_jobs():
    jobs = []
    for L in range(LAYERS):
        jobs += [("qk", L, mt, w, c) for mt in range(CJ) for w in range(2) for c in range(NC)]
        jobs += [("v", L, t) for t in range(NT)]
        for t in range(NT + 2):
            if t < NT:
                jobs.append(("on", L, t))
            if t >= 2:
                jobs.append(("wo", L, t - 2))
        if L == 1:
            jobs += [("ffnT", L, t) for t in range(NT)]
        jobs += [("up", L, c, ht) for c in range(NC) for ht in range(HT)]
        jobs += [("down", L, t) for t in range(NT)]
    return jobs


A_AT = {job: n for n, job in enumerate(ring_a_jobs())}
B_AT = {job: n for n, job in enumerate(ring_b_jobs())}


def max_items(c):
    items = []
    if c > 0:
        items += [(qt, 0, (h,), 0, CH * c) for qt in range(TPC) for h in range(G)]
    for qt in reversed(range(TPC)):
        keys = P * (qt + 1)
        per = CH // keys
        items += [(qt, 1, tuple(range(h, h + per)), CH * c, keys) for h in range(0, G, per)]
    return items


T_LAG = 3
LEAD = 22
RATIO = 3.6


def attention_order():
    entries = []
    waiting = []
    for cg in range(NC * NG):
        for n, it in enumerate(max_items(cg // NG)):
            entries.append(("max", cg, it))
            if waiting and n == T_LAG:
                entries.append(("turn", waiting.pop()))
        waiting.append(cg)
    entries.append(("turn", waiting.pop()))
    order, done = [], 0

    def upto(n):
        nonlocal done
        while done < min(n, len(entries)):
            order.append(entries[done])
            done += 1

    steps = exp_steps()
    turned = {e[1]: n + 1 for n, e in enumerate(entries) if e[0] == "turn"}
    for s, (cg, kt) in enumerate(steps):
        upto(max(int(LEAD + RATIO * s), turned[cg] + (3 if kt == 0 else 0)))
        order.append(("exp", s))
        if s >= 1:
            order.append(("pv", s - 1))
    upto(len(entries))
    order.append(("pv", len(steps) - 1))
    return order


def exp_steps():
    return [(cg, kt) for cg in range(NC * NG) for kt in range(TPC * (cg // NG + 1))]


STEPS = exp_steps()
ORDER = attention_order()
N_MAX = sum(e[0] in ("max", "turn") for e in ORDER)
LAST_STEP = {cg: max(s for s, x in enumerate(STEPS) if x[0] == cg) for cg in range(NC * NG)}


def step_span(s):
    cg, kt = STEPS[s]
    c, g = cg // NG, cg % NG
    return g, c, kt, max(kt * P - c * CH, 0), kt * P >= c * CH


def alibi_tail():
    bf16 = mybir.dt.np(BF16)
    start = 2.0 ** -0.5
    slopes = np.array([start * start ** i for i in range(NH)], np.float32)
    bias = slopes[:, None] * (np.arange(T, dtype=np.float32) - np.float32(T - 1))[None, :]
    rest = bias.astype(np.float32) / np.float32(SCALE)
    rows = []
    for _ in range(3):
        part = rest.astype(bf16)
        rows.append(part)
        rest = rest - part.astype(np.float32)
    rows += [np.ones((NH, T), bf16)] * MAX_ROWS
    return np.stack(rows)


def two_layer_kernel(nc, a, out, tail):
    with ExitStack() as ctx:
        def sb(name, shape, dt):
            return ctx.enter_context(nc.sbuf_tensor(name, shape, dt))

        def sem(name):
            return ctx.enter_context(nc.semaphore(name))

        ps = ctx.enter_context(nc.psum_tensor("ps", [P, 8, CH], F32))
        x = sb("x", [P, NT, C], F32)
        xn = sb("xn", [P, NT, C], F32)
        xnT = sb("xnT", [P, CJ, T], F32)
        xhl = xnT[:, :, :].bitcast(FP16).rearrange("p j (s t) -> p j s t", s=2)
        parts = sb("parts", [P, 4, 3, CH], BF16)
        rest = sb("rest", [P, 2, CH], F32)
        qS = sb("qS", [P, NH, T], BF16)
        kS = sb("kS", [P, NH, T], BF16)
        v1 = sb("v1", [P, NT, NH, 2 * HD], F32)
        prob = sb("prob", [P, 3, G, CH], F32)
        oT = sb("oT", [P, NG, T], F32)
        onT = sb("onT", [P, 2, CJ, P], F32)
        rec = sb("rec", [P, 2, NH], F32)
        mx = sb("mx", [P, 2, TPC, G, 2], F32)
        mm = sb("mm", [P, 2, TPC * G], F32)
        mneg = sb("mneg", [P, 2, 2, G, TPC], BF16)
        mT = sb("mT", [2 * G * TPC, 2, P], BF16)
        w0 = sb("w0", [P, 4, CJ, C], F32)
        w1r = oT[:, :, :].rearrange("p g t -> p (g t)")[:, 0:4 * CJ * C].rearrange(
            "p (m j i) -> p m j i", m=4, j=CJ)
        w1T = sb("w1T", [P, 4, CJ, C], F32)
        bqk = sb("bqk", [P, 2, CJ], F32)
        bv = sb("bv", [P, C], F32)
        bo = sb("bo", [P, C], F32)
        flat = prob[:, :, :, :].rearrange("p r g q -> p (r g q)")
        g0 = flat[:, 0:2 * HT * C].rearrange("p (m k i) -> p m k i", m=2, k=HT)
        d0 = flat[:, 2 * HT * C:2 * HT * C + CJ * HID0].rearrange("p (j i) -> p j i", j=CJ)
        s0 = sb("s0", [P, 2, HT], F32)
        sd0 = sb("sd0", [P, CJ], F32)
        gu0T = sb("gu0T", [P, 2, CJ, HID0], F32)
        d0T = sb("d0T", [P, HT, C], F32)
        w8 = gu0T[:, :, :, :].rearrange("p m j i -> p (m j i)")[:, 0:CJ * HID1]
        w8m = d0T[:, :, :].rearrange("p k i -> p (k i)")
        gu1 = sb("gu1", [P, 2, CJ, HID1], FP16)
        d1 = w0[:, :, :, :].rearrange("p m j i -> p (m j i)")[:, 0:HT * C].rearrange("p (k i) -> p k i", k=HT)
        s1 = sb("s1", [P, 2, HT], F32)
        sd1 = sb("sd1", [P, C], F32)
        stats = sb("stats", [P, NT, 6], F32)
        mv = sb("mv", [P, NT, 2], F32)
        ve = sb("ve", [P, NT], F32)
        rstd = sb("rstd", [P, NT], F32)
        nhalf = sb("nhalf", [P, NT], F32)
        ident = sb("ident", [P, P], F32)
        identb = sb("identb", [P, P], BF16)
        mask_q = sb("mask_q", [P, P], BF16)
        mask_k = sb("mask_k", [P, P], BF16)
        fT = qS[:, :, :].rearrange("p h t -> p (h t)").bitcast(F32)[:, 0:HT * T].rearrange(
            "p (k t) -> p k t", k=HT)
        sg = rest

        qk_dram = [nc.dram_tensor(f"qk_scratch{L}", [2, 3, C, T], BF16, kind="Internal").ap() for L in range(LAYERS)]
        m_dram = nc.dram_tensor("m_scratch", [LAYERS, NC * NG, 2 * G * TPC, P], BF16, kind="Internal").ap()

        x_in = [sem(f"x_in{h}") for h in range(2)]
        w0_in = sem("w0_in")
        b0_in = sem("b0_in")
        w1_in = sem("w1_in")
        ffn0_in = sem("ffn0_in")
        ffn1s_in = sem("ffn1s_in")
        w8_in = sem("w8_in")
        tail_in = sem("tail_in")
        a_full, a_free = sem("a_full"), sem("a_free")
        b_full, b_free = sem("b_full"), sem("b_free")
        s_full, s_free = sem("s_full"), sem("s_free")
        m_full, m_free = sem("m_full"), sem("m_free")
        pv_done, o_taken = sem("pv_done"), sem("o_taken")
        consts, consts_step = sem("consts"), sem("consts_step")
        stats_done, rstd_done, xn_done = sem("stats_done"), sem("rstd_done"), sem("xn_done")
        rstd_step = sem("rstd_step")
        dve_step = sem("dve_step")
        hi_done, mid_done, lo_done = sem("hi_done"), sem("mid_done"), sem("lo_done")
        saved = [sem(f"saved{k}") for k in range(4)]
        stacked = [sem(f"stacked{mt}") for mt in range(CJ)]
        mneg_done, mT_done, m_saved, m_stacked = sem("mneg_done"), sem("mT_done"), sem("m_saved"), sem("m_stacked")
        ones_k = sem("ones_k")
        ffn0_w, ffn0_d = sem("ffn0_w"), sem("ffn0_d")
        w8_exp, w8_round, w8_step = sem("w8_exp"), sem("w8_round"), sem("w8_step")
        x_biased = sem("x_biased")
        silu_done, f_done = sem("silu_done"), sem("f_done")
        fx_hi = sem("fx_hi")
        x_final = sem("x_final")
        stored = sem("stored")

        ctx.enter_context(nc.allow_non_contiguous_dma(reason="biases and scales, a few elements per partition"))
        block = ctx.enter_context(nc.Block())

        N_QK = CJ * 2 * NC
        N_STEP = len(STEPS)

        def attn_w(L, m):
            return w0[:, m] if L == 0 else w1T[:, m]

        @block.sync
        def _(sp):
            xin = a["L0_attn_x"].rearrange("o (t p) c -> p (o t) c", p=P)
            for h in range(2):
                sp.dma_start(x[:, 4 * h:4 * h + 4, :], xin[:, 4 * h:4 * h + 4, :]).then_inc(x_in[h], 16)
            sp.dma_start(kS[QK_ROWS:K_EXP[0], :, :], tail).then_inc(tail_in, 16)
            for m, n in enumerate(("Wq", "Wk", "Wv", "Wo")):
                sp.dma_start(w1r[:, m], a[f"L1_attn_{n}"].rearrange("(j p) i -> p j i", p=P)).then_inc(w1_in, 16)
            full = HID0 // P
            for m, n in enumerate(("gate", "up")):
                w = a[f"L0_ffn_wq_{n}"]
                sp.dma_start(g0[:, m, 0:full].bitcast(I32), w[0:full * P].rearrange("(k p) i -> p k i", p=P)).then_inc(ffn0_in, 16)
                sp.dma_start(g0[0:HID0 - full * P, m, full].bitcast(I32), w[full * P:HID0]).then_inc(ffn0_in, 16)
            sp.dma_start(d0[:, :, :].bitcast(I32), a["L0_ffn_wq_down"].rearrange("(j p) i -> p j i", p=P)).then_inc(ffn0_in, 16)
            for L in range(LAYERS):
                for mt in range(CJ):
                    for n in range(4):
                        job = L * N_QK + mt * 4 + n
                        w, c = n // NC, n % NC
                        sp.wait_ge(lo_done, job + 1)
                        dst = qk_dram[L][w, :, mt * P:(mt + 1) * P, c * CH:(c + 1) * CH].rearrange("s p t -> p s t")
                        sp.dma_start(dst, parts[:, n]).then_inc(saved[n], 16)
                    for n in range(4):
                        sp.wait_ge(saved[n], 16 * (L * CJ + mt + 1))
                    heads = NH // CJ
                    for w, (stack, order) in enumerate(((qS, Q_PARTS), (kS, K_PARTS))):
                        for r, part in enumerate(order):
                            src = qk_dram[L][w, part, mt * P:(mt + 1) * P, :].rearrange("(h d) t -> d h t", d=HD)
                            sp.dma_start(stack[r * HD:(r + 1) * HD, mt * heads:(mt + 1) * heads, :], src).then_inc(stacked[mt], 16)
                for cg in range(NC * NG):
                    c, g = cg // NG, cg % NG
                    n = L * NC * NG + cg
                    sp.wait_ge(mT_done, n + 1)
                    sp.dma_start(m_dram[L, cg], mT[:, cg % 2, :]).then_inc(m_saved, 16)
                    sp.wait_ge(m_saved, 16 * (n + 1))
                    dst = qS[K_MAX[L]:K_EXP[L], g * G:(g + 1) * G, c * CH:(c + 1) * CH]
                    src = m_dram[L, cg].rearrange("(s h t) q -> s h (t q)", s=2, h=G)
                    if n:
                        sp.wait_ge(m_stacked, 16 * n)
                    sp.dma_start(dst, src).then_inc(m_stacked, 16)
            yout = out.rearrange("o (t p) c -> p (o t) c", p=P)
            for t in range(NT):
                sp.wait_ge(x_final, t + 1)
                sp.dma_start(yout[:, t, :], x[:, t, :]).then_inc(stored, 16)
            sp.wait_ge(stored, 16 * NT)

        @block.gpsimd
        def _(pool):
            k = [0]

            def chain(ins):
                ins.then_inc(consts_step, 1)
                k[0] += 1
                pool.wait_ge(consts_step, k[0])

            nc.gpsimd.memset(nhalf[:], -0.5)
            nc.gpsimd.memset(ident[:], 0.0)
            nc.gpsimd.memset(identb[:], 0.0)
            nc.gpsimd.memset(mask_q[:], 0.0)
            chain(nc.gpsimd.memset(mask_k[:], 0.0))
            for m in (ident, identb):
                nc.gpsimd.affine_select(out=m[:], in_=m[:], compare_op=ALU.not_equal, fill=1.0, base=0,
                                        pattern=[[-1, P]], channel_multiplier=1)
            nc.gpsimd.affine_select(out=mask_q[:], in_=mask_q[:], compare_op=ALU.is_ge, fill=NEG, base=0,
                                    pattern=[[-1, P]], channel_multiplier=1)
            nc.gpsimd.affine_select(out=mask_k[:], in_=mask_k[:], compare_op=ALU.is_ge, fill=NEG, base=0,
                                    pattern=[[1, P]], channel_multiplier=-1).then_inc(consts, 1)

            def rstd_of(n):
                half = slice(4 * (n % 2), 4 * (n % 2) + 4)
                pool.wait_ge(stats_done, n + 1)
                nc.gpsimd.tensor_scalar(ve[:, half], mv[:, half, 1], EPS, None, ALU.add).then_inc(rstd_step, 1)
                pool.wait_ge(rstd_step, n + 1)
                nc.gpsimd.tensor_tensor(rstd[:, half], ve[:, half], nhalf[:, half], ALU.pow).then_inc(rstd_done, 1)

            rstd_of(0)
            rstd_of(1)
            pool.wait_ge(rstd_done, 2)
            chain(nc.gpsimd.memset(qS[QK_ROWS:QK_ROWS + ALIBI_ROWS[0], :, :], 1.0))
            nc.gpsimd.memset(v1[:, :, :, HD:2 * HD], 1.0).then_inc(consts, 1)
            pool.wait_ge(ffn0_in, 16 * 10)
            for m in range(2):
                for ht in range(HT):
                    r = hid_rows(0, ht)
                    w = g0[0:r, m, ht]
                    if m * HT + ht and (r < P or ht == 0):
                        pool.wait_ge(ffn0_w, m * HT + ht)
                    nc.gpsimd.tensor_scalar(w, w.bitcast(I32), -ZERO_POINT, s0[0:r, m, ht:ht + 1], ALU.add, ALU.mult).then_inc(ffn0_w, 1)
            pool.wait_ge(ffn0_w, 2 * HT)
            for j in range(CJ):
                nc.gpsimd.tensor_scalar(d0[:, j], d0[:, j].bitcast(I32), -ZERO_POINT, sd0[:, j:j + 1], ALU.add, ALU.mult).then_inc(ffn0_w, 1)
            pool.wait_ge(xn_done, NT)
            pool.wait_ge(b0_in, 16 * 4)
            for t in range(NT):
                nc.gpsimd.tensor_tensor(x[:, t], x[:, t], bo[:], ALU.add).then_inc(x_biased, 1)

            rstd_of(2)
            rstd_of(3)
            pool.wait_ge(b_full, B_AT["on", 0, 0] + 1)
            pool.wait_ge(rstd_done, 4)
            nc.gpsimd.memset(kS[K_MAX[1]:K_EXP[1], :, :], 1.0).then_inc(ones_k, 1)
            pool.wait_ge(ones_k, 1)
            rstd_of(4)
            rstd_of(5)
            pool.wait_ge(ffn1s_in, 16 * 3)
            w8_src = [a["L1_ffn_gate_w"].rearrange("(j p) i -> p j i", p=P),
                      a["L1_ffn_up_w"].rearrange("(j p) i -> p j i", p=P),
                      a["L1_ffn_down_w"].rearrange("(k p) i -> p k i", p=P)]
            for n in range(3):
                if n:
                    pool.wait_ge(w8_round, n)
                pool.dma_start(w8.rearrange("p (j i) -> p j i", j=w8_src[n].shape[1]), w8_src[n]).then_inc(w8_in, 16)
                pool.wait_ge(w8_exp, n + 1)
                chain(nc.gpsimd.tensor_scalar(w8m[:], w8m[:], 2.0 ** -6, 1.5 * 2.0 ** 20, ALU.max, ALU.mult))
                chain(nc.gpsimd.tensor_tensor(w8, w8, w8m[:], ALU.add))
                chain(nc.gpsimd.tensor_tensor(w8, w8, w8m[:], ALU.subtract))
                chain(nc.gpsimd.tensor_scalar(w8m[:], w8, 0.55 * 2.0 ** 120, 0.0, ALU.mult, ALU.mult))
                if n < 2:
                    dst = gu1[:, n].rearrange("p j i -> p (j i)")
                    nc.gpsimd.tensor_tensor(dst, w8, w8m[:], ALU.add).then_inc(w8_round, 1)
                else:
                    dst = d1[:, :, :].rearrange("p k i -> p (k i)")
                    chain(nc.gpsimd.tensor_tensor(dst, w8, w8m[:], ALU.add))
                    for ht in range(HT):
                        ins = nc.gpsimd.tensor_tensor(d1[:, ht], d1[:, ht], sd1[:], ALU.mult)
                    ins.then_inc(w8_round, 1)
            rstd_of(6)
            rstd_of(7)

        @block.tensor
        def _(pe):
            def take_a(job):
                n = A_AT[job]
                if n >= 4:
                    pe.wait_ge(a_free, n - 3)
                return ps[:, n % 4]

            def take_b(job):
                n = B_AT[job]
                if n >= 4:
                    pe.wait_ge(b_free, n - 3)
                return ps[:, 4 + n % 4]

            def ln_transposes(job, ln, L, take, full):
                for t in range(NT):
                    bank = take((job, L, t))
                    pe.wait_ge(xn_done, ln * NT + t + 1)
                    for j in range(CJ):
                        mmi = nc.tensor.transpose(bank[:, j * P:(j + 1) * P], xn[:, t, j * P:(j + 1) * P], ident[:])
                    mmi.then_inc(full, 1)

            def weight_transposes():
                pe.wait_ge(w1_in, 16 * 4)
                for m in range(4):
                    bank = take_a(("w1T", m))
                    for jo in range(CJ):
                        for ji in range(CJ):
                            mmi = nc.tensor.transpose(bank[:, ji * C + jo * P:ji * C + (jo + 1) * P],
                                                      w1r[:, m, jo, ji * P:(ji + 1) * P], ident[:])
                    mmi.then_inc(a_full, 1)
                for m, name in enumerate(("gateT", "upT")):
                    for k in range(HT // 2):
                        bank = take_a((name, k))
                        pe.wait_ge(ffn0_w, m * HT + 2 * k + 2)
                        for i in range(2):
                            r = hid_rows(0, 2 * k + i)
                            for j in range(CJ):
                                mmi = nc.tensor.transpose(bank[:, j * C + i * P:j * C + i * P + r],
                                                          g0[0:r, m, 2 * k + i, j * P:(j + 1) * P], ident[0:r, 0:r])
                        mmi.then_inc(a_full, 1)
                pe.wait_ge(ffn0_w, 2 * HT + CJ)
                for k in range(HT // 2):
                    bank = take_a(("downT", k))
                    for i in range(2):
                        r = hid_rows(0, 2 * k + i)
                        for j in range(CJ):
                            mmi = nc.tensor.transpose(bank[0:r, i * C + j * P:i * C + (j + 1) * P],
                                                      d0[:, j, (2 * k + i) * P:(2 * k + i) * P + r], ident[:])
                    mmi.then_inc(a_full, 1)

            def max_scores(L, n, cg, item):
                c, g = cg // NG, cg % NG
                qt, part, heads, key0, keys = item
                bank = ps[:, 4 + n % 2]
                q0 = c * CH + qt * P
                for i, h in enumerate(heads):
                    span = bank[:, i * keys:(i + 1) * keys]
                    mmi = nc.tensor.matmul(span, qS[0:K_MAX[L], g * G + h, q0:q0 + P],
                                           kS[0:K_MAX[L], g * G + h, key0:key0 + keys], start=True, stop=part == 0)
                    if part == 1:
                        mmi = nc.tensor.matmul(span[:, keys - P:keys], identb[:], mask_q[:], start=False, stop=True)
                mmi.then_inc(m_full, 1)

            def exp_scores(L, s):
                g, c, kt, off, diagonal = step_span(s)
                q0 = c * CH
                for pair in range(G // 2):
                    n = 2 * (L * N_STEP + s) + pair
                    if n >= 2:
                        pe.wait_ge(s_free, n - 1)
                    for i in range(2):
                        h = g * G + 2 * pair + i
                        bank = ps[:, 2 * (n % 2) + i]
                        mmi = nc.tensor.matmul(bank[:, off:CH], kS[0:K_EXP[L], h, kt * P:(kt + 1) * P],
                                               qS[0:K_EXP[L], h, q0 + off:q0 + CH], start=True, stop=not diagonal)
                        if diagonal:
                            mmi = nc.tensor.matmul(bank[:, off:off + P], identb[:], mask_k[:], start=False, stop=True)
                    mmi.then_inc(s_full, 1)

            def times_v(L, s):
                g, c, kt, off, _ = step_span(s)
                cg = STEPS[s][0]
                n = L * N_STEP + s
                pe.wait_ge(s_free, 2 * (n + 1))
                if kt == 0 and L * NC * NG + cg >= 2:
                    pe.wait_ge(o_taken, L * NC * NG + cg - 1)
                bank = ps[:, 6 + cg % 2]
                for h in range(G):
                    mmi = nc.tensor.matmul(bank[32 * h:32 * h + 32, off:CH], v1[:, kt, g * G + h, :],
                                           prob[:, n % 3, h, off:CH], start=kt == 0, stop=s == LAST_STEP[cg])
                mmi.then_inc(pv_done, 1)

            def attention(L):
                m_n = L * N_MAX
                pe.wait_ge(a_free, A_AT["onT", L, 0])
                pe.wait_ge(b_free, B_AT["on", L, 0])
                loaded = set()
                for entry in ORDER:
                    if entry[0] == "max":
                        _, cg, item = entry
                        mt = cg % NG // 2
                        if mt not in loaded:
                            pe.wait_ge(stacked[mt], 16 * 12 * (L + 1))
                            loaded.add(mt)
                        if m_n >= 2:
                            pe.wait_ge(m_free, m_n - 1)
                        max_scores(L, m_n, cg, item)
                        m_n += 1
                    elif entry[0] == "turn":
                        cg = entry[1]
                        pe.wait_ge(m_free, m_n - 1)
                        pe.wait_ge(mneg_done, L * NC * NG + cg + 1)
                        nc.tensor.transpose(ps[0:2 * G * TPC, 4 + m_n % 2, 0:P // 2].bitcast(BF16),
                                            mneg[:, cg % 2].rearrange("p s h t -> p (s h t)"), identb[:]).then_inc(m_full, 1)
                        m_n += 1
                    elif entry[0] == "exp":
                        cg, kt = STEPS[entry[1]]
                        if kt == 0:
                            pe.wait_ge(m_stacked, 16 * (L * NC * NG + cg + 1))
                        exp_scores(L, entry[1])
                    else:
                        times_v(L, entry[1])

            def out_projection(L):
                pe.wait_ge(m_free, (L + 1) * N_MAX)
                pe.wait_ge(o_taken, (L + 1) * NC * NG)
                pe.wait_ge(s_free, 2 * (L + 1) * N_STEP)
                for t in range(NT + 2):
                    if t < NT:
                        bank = take_b(("on", L, t))
                        for g in range(NG):
                            mmi = nc.tensor.transpose(bank[:, g * P:(g + 1) * P], oT[:, g, t * P:(t + 1) * P], ident[:])
                        mmi.then_inc(b_full, 1)
                    if 1 <= t <= NT:
                        bank = take_a(("onT", L, t - 1))
                        pe.wait_ge(b_free, B_AT["on", L, t - 1] + 1)
                        for j in range(CJ):
                            mmi = nc.tensor.transpose(bank[:, j * P:(j + 1) * P], xn[:, t - 1, j * P:(j + 1) * P], ident[:])
                        mmi.then_inc(a_full, 1)
                    if t >= 2:
                        bank = take_b(("wo", L, t - 2))
                        pe.wait_ge(a_free, A_AT["onT", L, t - 2] + 1)
                        for j in range(CJ):
                            mmi = nc.tensor.matmul(bank[:, 0:C], onT[:, t % 2, j], attn_w(L, 3)[:, j, :], start=j == 0, stop=j == CJ - 1)
                        mmi.then_inc(b_full, 1)

            def ffn(L):
                for c in range(NC):
                    for ht in range(HT):
                        r = hid_rows(L, ht)
                        for m, (name, take, full) in enumerate((("gate", take_a, a_full), ("up", take_b, b_full))):
                            bank = take((name, L, c, ht))
                            if L == 0 and ht == 0:
                                pe.wait_ge(a_free, A_AT["ffnT", L, (c + 1) * TPC - 1] + 1)
                            if L == 1 and ht == 0:
                                pe.wait_ge(b_free, B_AT["ffnT", L, (c + 1) * TPC - 1] + 1)
                            if L == 0:
                                for j in range(CJ):
                                    mmi = nc.tensor.matmul(bank[0:r, :], gu0T[:, m, j, ht * P:ht * P + r],
                                                           xnT[:, j, c * CH:(c + 1) * CH], start=j == 0, stop=j == CJ - 1)
                            else:
                                for j in range(CJ):
                                    for s in range(2):
                                        mmi = nc.tensor.matmul(bank[:, :], gu1[:, m, j, ht * P:(ht + 1) * P],
                                                               xhl[:, j, s, c * CH:(c + 1) * CH],
                                                               start=j + s == 0, stop=j == CJ - 1 and s == 1)
                            mmi.then_inc(full, 1)
                for t in range(NT):
                    bank = take_b(("down", L, t))
                    pe.wait_ge(f_done, (L * NC + t // TPC + 1) * HT)
                    if L == 1 and t == 0:
                        pe.wait_ge(w8_round, 3)
                    for ht in range(HT):
                        r = hid_rows(L, ht)
                        w = d0T if L == 0 else d1
                        mmi = nc.tensor.matmul(bank[:, 0:C], fT[0:r, ht, t * P:(t + 1) * P], w[0:r, ht, :],
                                               start=ht == 0, stop=ht == HT - 1)
                    mmi.then_inc(b_full, 1)

            pe.wait_ge(consts, 1)
            for L in range(LAYERS):
                ln_transposes("xnT", 2 * L, L, take_a, a_full)
                if L == 0:
                    pe.wait_ge(w0_in, 16 * 4)
                for mt in range(CJ):
                    for w in range(2):
                        for c in range(NC):
                            bank = take_b(("qk", L, mt, w, c))
                            pe.wait_ge(a_free, A_AT["xnT", L, (c + 1) * TPC - 1] + 1)
                            for j in range(CJ):
                                mmi = nc.tensor.matmul(bank[:, :], attn_w(L, w)[:, j, mt * P:(mt + 1) * P],
                                                       xnT[:, j, c * CH:(c + 1) * CH], start=j == 0, stop=j == CJ - 1)
                            mmi.then_inc(b_full, 1)
                if L == 0:
                    pe.wait_ge(consts, 2)
                for t in range(NT):
                    bank = take_b(("v", L, t))
                    for j in range(CJ):
                        mmi = nc.tensor.matmul(bank[:, 0:C], xnT[:, j, t * P:(t + 1) * P], attn_w(L, 2)[:, j, :],
                                               start=j == 0, stop=j == CJ - 1)
                    mmi.then_inc(b_full, 1)
                if L == 0:
                    weight_transposes()
                    pe.wait_ge(tail_in, 16)
                else:
                    pe.wait_ge(ones_k, 1)
                attention(L)
                out_projection(L)
                ln_transposes("ffnT", 2 * L + 1, L, take_a if L == 0 else take_b, a_full if L == 0 else b_full)
                if L == 1:
                    pe.wait_ge(w8_round, 2)
                ffn(L)

        @block.scalar
        def _(act):
            for m, n in enumerate(("Wq", "Wk", "Wv", "Wo")):
                act.dma_start(w0[:, m], a[f"L0_attn_{n}"].rearrange("(j p) o -> p j o", p=P)).then_inc(w0_in, 16)
            for m, n in enumerate(("bq", "bk")):
                act.dma_start(bqk[:, m], a[f"L0_attn_{n}"].rearrange("(j p) -> p j", p=P)).then_inc(b0_in, 16)
            act.dma_start(bv[:], a["L0_attn_bv"].unsqueeze(0).to_broadcast([P, C])).then_inc(b0_in, 16)
            act.dma_start(bo[:], a["L0_attn_bo"].unsqueeze(0).to_broadcast([P, C])).then_inc(b0_in, 16)
            full = HID0 // P
            for m, n in enumerate(("gate", "up")):
                s = a[f"L0_ffn_s_{n}"]
                act.dma_start(s0[:, m, 0:full], s[0:full * P].rearrange("(k p) -> p k", p=P)).then_inc(ffn0_in, 16)
                act.dma_start(s0[0:HID0 - full * P, m, full:full + 1], s[full * P:HID0].unsqueeze(1)).then_inc(ffn0_in, 16)
                act.dma_start(s1[:, m], a[f"L1_ffn_{n}_scale"].rearrange("(k p) -> p k", p=P)).then_inc(ffn1s_in, 16)
            act.dma_start(sd0[:], a["L0_ffn_s_down"].rearrange("(j p) -> p j", p=P)).then_inc(ffn0_in, 16)
            act.dma_start(sd1[:], a["L1_ffn_down_scale"].unsqueeze(0).to_broadcast([P, C])).then_inc(ffn1s_in, 16)

            def bank_a(job):
                n = A_AT[job]
                act.wait_ge(a_full, n + 1)
                return ps[:, n % 4]

            def drain_transposed(job, L):
                for t in range(NT):
                    bank = bank_a((job, L, t))
                    nc.scalar.copy(xnT[:, :, t * P:(t + 1) * P], bank[:, 0:C].rearrange("p (j t) -> p j t", j=CJ)).then_inc(a_free, 1)

            def qk_parts(L):
                for n in range(N_QK + 1):
                    if n < N_QK:
                        mt, w, c = n // 4, n // 2 % 2, n % 2
                        job = B_AT["qk", L, mt, w, c]
                        act.wait_ge(b_full, job + 1)
                        if L * N_QK + n >= 4:
                            act.wait_ge(saved[n % 4], 16 * (L * CJ + mt))
                        bias = bqk[:, w, mt:mt + 1] if L == 0 else 0.0
                        nc.scalar.activation(parts[:, n % 4, 0], ps[:, 4 + job % 4], ACT.Identity, bias=bias).then_inc(hi_done, 1)
                    if n >= 1:
                        m = n - 1
                        act.wait_ge(b_free, B_AT["qk", L, m // 4, m // 2 % 2, m % 2] + 1)
                        nc.scalar.copy(parts[:, m % 4, 1], rest[:, m % 2]).then_inc(mid_done, 1)

            for L in range(LAYERS):
                drain_transposed("xnT", L)
                if L == 0:
                    act.wait_ge(b0_in, 16 * 4)
                qk_parts(L)
                if L == 0:
                    for m in range(4):
                        bank = bank_a(("w1T", m))
                        nc.scalar.copy(w1T[:, m].rearrange("p j o -> p (j o)"), bank).then_inc(a_free, 1)
                    for m, name in enumerate(("gateT", "upT")):
                        for k in range(HT // 2):
                            bank = bank_a((name, k))
                            w = hid_rows(0, 2 * k) + hid_rows(0, 2 * k + 1)
                            nc.scalar.copy(gu0T[:, m, :, 2 * k * P:2 * k * P + w],
                                           bank.rearrange("p (j o) -> p j o", j=CJ)[:, :, 0:w]).then_inc(a_free, 1)
                    for k in range(HT // 2):
                        bank = bank_a(("downT", k))
                        r = hid_rows(0, 2 * k + 1)
                        if r == P:
                            nc.scalar.copy(d0T[:, 2 * k:2 * k + 2].rearrange("p k o -> p (k o)"), bank).then_inc(a_free, 1)
                        else:
                            nc.scalar.copy(d0T[:, 2 * k], bank[:, 0:C])
                            nc.scalar.copy(d0T[0:r, 2 * k + 1], bank[0:r, C:2 * C]).then_inc(a_free, 1)
                for s in range(N_STEP):
                    off = step_span(s)[3]
                    n = L * N_STEP + s
                    if n >= 3:
                        act.wait_ge(pv_done, n - 2)
                    for pair in range(G // 2):
                        m = 2 * n + pair
                        act.wait_ge(s_full, m + 1)
                        nc.scalar.activation(prob[:, n % 3, 2 * pair:2 * pair + 2, off:CH],
                                             ps[:, 2 * (m % 2):2 * (m % 2) + 2, off:CH], ACT.Exp, scale=SCALE).then_inc(s_free, 1)
                for t in range(NT):
                    bank = bank_a(("onT", L, t))
                    if t >= 2:
                        act.wait_ge(b_full, B_AT["wo", L, t - 2] + 1)
                    nc.scalar.copy(onT[:, t % 2].rearrange("p j q -> p (j q)"), bank[:, 0:C]).then_inc(a_free, 1)
                if L == 0:
                    drain_transposed("ffnT", L)
                else:
                    for t in range(NT):
                        job = B_AT["ffnT", L, t]
                        act.wait_ge(b_full, job + 1)
                        nc.scalar.copy(xhl[:, :, 0, t * P:(t + 1) * P],
                                       ps[:, 4 + job % 4, 0:C].rearrange("p (j t) -> p j t", j=CJ)).then_inc(fx_hi, 1)
                    act.wait_ge(ffn1s_in, 16 * 3)
                for c in range(NC):
                    for ht in range(HT):
                        r = hid_rows(L, ht)
                        n = (L * NC + c) * HT + ht
                        bank = bank_a(("gate", L, c, ht))
                        if n >= 2:
                            act.wait_ge(f_done, n - 1)
                        scale = 1.0 if L == 0 else s1[:, 0, ht:ht + 1]
                        nc.scalar.activation(sg[0:r, n % 2], bank[0:r], ACT.Silu, scale=scale).then_inc(a_free, 1)

        @block.vector
        def _(dve):
            k = [0]

            def chain(ins):
                ins.then_inc(dve_step, 1)
                k[0] += 1

            def settle():
                dve.wait_ge(dve_step, k[0])

            def bank_b(job):
                n = B_AT[job]
                dve.wait_ge(b_full, n + 1)
                return ps[:, 4 + n % 4]

            def ln_stats(t):
                chain(nc.vector.bn_stats(stats[:, t], x[:, t]))
                settle()
                ins = nc.vector.bn_aggr(mv[:, t], stats[:, t])
                if t % 4 == 3:
                    ins.then_inc(stats_done, 1)

            def ln_normalise(ln):
                for half in range(2):
                    dve.wait_ge(rstd_done, 2 * ln + half + 1)
                    dve.wait_ge(stats_done, 2 * ln + half + 1)
                    for t in range(4 * half, 4 * half + 4):
                        nc.vector.tensor_scalar(xn[:, t], x[:, t], mv[:, t, 0:1], rstd[:, t:t + 1],
                                                ALU.subtract, ALU.mult).then_inc(xn_done, 1)

            def round_w8(n):
                dve.wait_ge(w8_in, 16 * (n + 1))
                if n:
                    dve.wait_ge(w8_round, n)
                nc.vector.tensor_scalar(w8m[:].bitcast(I32), w8.bitcast(I32), 0x7F800000, None, ALU.bitwise_and).then_inc(w8_exp, 1)

            def add_to_x(job, L, t, last=False):
                bank = bank_b((job, L, t))
                ins = nc.vector.tensor_tensor(x[:, t], bank[:, 0:C], x[:, t], ALU.add)
                return ins

            def attention(L):
                m_n = L * N_MAX
                left = {}
                for entry in ORDER:
                    if entry[0] == "max":
                        _, cg, (qt, part, heads, key0, keys) = entry
                        slot = cg % 2
                        dve.wait_ge(m_full, m_n + 1)
                        src = ps[:, 4 + m_n % 2, 0:len(heads) * keys].rearrange("p (h k) -> p h k", h=len(heads))
                        ins = nc.vector.tensor_reduce(mx[:, slot, qt, heads[0]:heads[-1] + 1, part], src, AX_X, ALU.max)
                        ins.then_inc(m_free, 1)
                        m_n += 1
                        left[cg] = left.get(cg, len(max_items(cg // NG))) - 1
                        if left[cg] == 0:
                            negate_max(L, cg, m_n)
                    elif entry[0] == "turn":
                        n = L * NC * NG + entry[1]
                        dve.wait_ge(m_full, m_n + 1)
                        if n >= 2:
                            dve.wait_ge(m_saved, 16 * (n - 1))
                        nc.vector.tensor_copy(mT[:, entry[1] % 2], ps[0:2 * G * TPC, 4 + m_n % 2, 0:P // 2].bitcast(BF16)).then_inc(mT_done, 1)
                        dve.wait_ge(mT_done, n + 1)
                        nc.vector.engine_nop().then_inc(m_free, 1)
                        m_n += 1
                        if L == 1 and entry[1] in (3, 4):
                            round_w8(entry[1] - 2)
                    elif entry[0] == "pv" and entry[1] == LAST_STEP[STEPS[entry[1]][0]]:
                        cg = STEPS[entry[1]][0]
                        dve.wait_ge(pv_done, L * N_STEP + entry[1] + 1)
                        c, g = cg // NG, cg % NG
                        nc.vector.tensor_copy(oT[:, g, c * CH:(c + 1) * CH], ps[:, 6 + cg % 2]).then_inc(o_taken, 1)

            def negate_max(L, cg, m_n):
                slot = cg % 2
                dve.wait_ge(m_free, m_n)
                both = mx[:, slot].rearrange("p t h s -> p (t h) s")
                if cg >= NG:
                    chain(nc.vector.tensor_tensor(mm[:, slot], both[:, :, 0], both[:, :, 1], ALU.max))
                    settle()
                    top = mm[:, slot].rearrange("p (t h) -> p h t", h=G)
                else:
                    top = both[:, :, 1].rearrange("p (t h) -> p h t", h=G)
                chain(nc.vector.tensor_scalar(mneg[:, slot, 0], top, -1.0, None, ALU.mult))
                settle()
                nc.vector.scalar_tensor_tensor(mneg[:, slot, 1], top, -1.0, mneg[:, slot, 0],
                                               ALU.mult, ALU.subtract).then_inc(mneg_done, 1)

            for h in range(2):
                dve.wait_ge(x_in[h], 16)
                for t in range(4 * h, 4 * h + 4):
                    ln_stats(t)
            for L in range(LAYERS):
                ln_normalise(2 * L)
                if L == 0:
                    dve.wait_ge(b0_in, 16 * 4)
                for n in range(N_QK + 1):
                    if n < N_QK:
                        mt, w, c = n // 4, n // 2 % 2, n % 2
                        bank = bank_b(("qk", L, mt, w, c))
                        dve.wait_ge(hi_done, L * N_QK + n + 1)
                        if L * N_QK + n >= 2:
                            dve.wait_ge(lo_done, L * N_QK + n - 1)
                        bias = bqk[:, w, mt:mt + 1] if L == 0 else 0.0
                        nc.vector.scalar_tensor_tensor(rest[:, n % 2], bank, bias, parts[:, n % 4, 0],
                                                       ALU.add, ALU.subtract).then_inc(b_free, 1)
                    if n >= 1:
                        m = n - 1
                        dve.wait_ge(mid_done, L * N_QK + m + 1)
                        nc.vector.tensor_tensor(parts[:, m % 4, 2], rest[:, m % 2], parts[:, m % 4, 1], ALU.subtract).then_inc(lo_done, 1)
                for t in range(NT):
                    bank = bank_b(("v", L, t))[:, 0:C].rearrange("p (h d) -> p h d", h=NH)
                    if L == 0:
                        ins = nc.vector.tensor_tensor(v1[:, t, :, 0:HD], bank, bv[:].rearrange("p (h d) -> p h d", h=NH), ALU.add)
                    else:
                        ins = nc.vector.tensor_copy(v1[:, t, :, 0:HD], bank)
                    ins.then_inc(b_free, 1)
                if L == 1:
                    round_w8(0)
                attention(L)
                if L == 0:
                    dve.wait_ge(x_biased, NT)
                for t in range(NT + 2):
                    if t < NT:
                        bank = bank_b(("on", L, t)).rearrange("p (h d) -> p h d", h=NH)
                        chain(nc.vector.reciprocal(rec[:, t % 2].unsqueeze(2), bank[:, :, HD:HD + 1]))
                        settle()
                        nc.vector.tensor_tensor(xn[:, t].rearrange("p (h d) -> p h d", h=NH), bank[:, :, 0:HD],
                                                rec[:, t % 2].unsqueeze(2).to_broadcast([P, NH, HD]), ALU.mult).then_inc(b_free, 1)
                    if t >= 2:
                        add_to_x("wo", L, t - 2).then_inc(b_free, 1)
                        dve.wait_ge(b_free, B_AT["wo", L, t - 2] + 1)
                        ln_stats(t - 2)
                ln_normalise(2 * L + 1)
                if L == 1:
                    for t in range(NT):
                        bank = bank_b(("ffnT", L, t))[:, 0:C].rearrange("p (j t) -> p j t", j=CJ)
                        dve.wait_ge(fx_hi, t + 1)
                        nc.vector.tensor_tensor(xhl[:, :, 1, t * P:(t + 1) * P], bank, xhl[:, :, 0, t * P:(t + 1) * P],
                                                ALU.subtract).then_inc(b_free, 1)
                for c in range(NC):
                    for ht in range(HT):
                        r = hid_rows(L, ht)
                        n = (L * NC + c) * HT + ht
                        bank = bank_b(("up", L, c, ht))
                        dve.wait_ge(a_free, A_AT["gate", L, c, ht] + 1)
                        f = fT[0:r, ht, c * CH:(c + 1) * CH]
                        if L == 0:
                            ins = nc.vector.tensor_tensor(f, bank[0:r], sg[0:r, n % 2], ALU.mult)
                        else:
                            ins = nc.vector.scalar_tensor_tensor(f, bank[0:r], s1[:, 1, ht:ht + 1], sg[:, n % 2], ALU.mult, ALU.mult)
                        ins.then_inc(f_done, 1)
                        dve.wait_ge(f_done, n + 1)
                        nc.vector.engine_nop().then_inc(b_free, 1)
                for t in range(NT):
                    ins = add_to_x("down", L, t)
                    if L == 0:
                        ins.then_inc(b_free, 1)
                        dve.wait_ge(b_free, B_AT["down", L, t] + 1)
                        ln_stats(t)
                    else:
                        ins.then_inc(x_final, 1)
                        if t < NT - 4:
                            dve.wait_ge(x_final, t + 1)
                            nc.vector.engine_nop().then_inc(b_free, 1)


_INS = ["L0_attn_x", "L0_attn_Wq", "L0_attn_bq", "L0_attn_Wk", "L0_attn_bk", "L0_attn_Wv", "L0_attn_bv", "L0_attn_Wo",
        "L0_attn_bo", "L0_ffn_wq_gate", "L0_ffn_s_gate", "L0_ffn_wq_up", "L0_ffn_s_up", "L0_ffn_wq_down",
        "L0_ffn_s_down", "L1_attn_Wq", "L1_attn_Wk", "L1_attn_Wv", "L1_attn_Wo", "L1_ffn_gate_w", "L1_ffn_up_w",
        "L1_ffn_down_w", "L1_ffn_gate_scale", "L1_ffn_up_scale", "L1_ffn_down_scale"]


def kernel(**inputs):
    import concourse.bacc as bacc
    from concourse.bass_utils import run_bass_kernel_spmd

    nc = bacc.Bacc("TRN2", target_bir_lowering=False, num_devices=1)
    arrays, aps = {}, {}
    for name in _INS:
        arr = np.ascontiguousarray(inputs[name])
        arrays[f"in_{name}"] = arr
        aps[name] = nc.dram_tensor(f"in_{name}", arr.shape, mybir.dt.from_np(arr.dtype), kind="ExternalInput").ap()
    arrays["alibi_tail"] = alibi_tail()
    tail = nc.dram_tensor("alibi_tail", arrays["alibi_tail"].shape, BF16, kind="ExternalInput").ap()
    out = nc.dram_tensor("out", (1, T, C), F32, kind="ExternalOutput").ap()
    two_layer_kernel(nc, aps, out, tail)
    r = run_bass_kernel_spmd(nc, [arrays], core_ids=[0])
    return r.results[0]["out"]
```

```python
from contextlib import ExitStack

import numpy as np

import concourse.bass as bass
from concourse import mybir

P = 128
T, C = 1024, 256
NH, HD = 16, 16
HID0, HID1 = 704, 768
NT = T // P
CH = 512
NC = T // CH
CJ = C // P
G = 4
NG = NH // G
TPC = CH // P
LAYERS = 2
HT = 6
NEG = -3.0e38
EPS = 1e-5
ZERO_POINT = 128.0
SCALE = float(HD) ** -0.5

F32, BF16, FP16, I32 = mybir.dt.float32, mybir.dt.bfloat16, mybir.dt.float16, mybir.dt.int32
ALU = mybir.AluOpType
ACT = mybir.ActivationFunctionType
AX_X = mybir.AxisListType.X

Q_PARTS = (0, 0, 0, 1, 1, 2)
K_PARTS = (2, 0, 1, 0, 1, 0)
QK_ROWS = len(Q_PARTS) * HD
ALIBI_ROWS = (3, 0)
MAX_ROWS = 2
K_MAX = [QK_ROWS + a for a in ALIBI_ROWS]
K_EXP = [k + MAX_ROWS for k in K_MAX]


def qk_job(n):
    return n // (2 * NC), n // 2 % NC, n % 2


N_QK = CJ * NC * 2


def hid_rows(layer, ht):
    return min(P, (HID0, HID1)[layer] - ht * P)



def ring_a_jobs():
    jobs = []
    for L in range(LAYERS):
        jobs += [("xnT", L, t) for t in range(NT)]
        jobs += [("v", L, t) for t in range(NT)]
        if L == 0:
            jobs += [("w1T", m) for m in range(4)]
            jobs += [(w, k) for w in ("gateT", "upT", "downT") for k in range(HT // 2)]
        jobs += [("onT", L, t) for t in range(NT)]
        if L == 0:
            jobs += [("ffnT", L, t) for t in range(NT)]
        jobs += [("gate", L, c, ht) for c in range(NC) for ht in range(HT)]
    return jobs


def ring_b_jobs():
    jobs = []
    for L in range(LAYERS):
        jobs += [("qk", L, n) for n in range(N_QK)]
        if L == 0:
            jobs.append(("bias",))
        for t in range(NT + 2):
            if t < NT:
                jobs.append(("on", L, t))
            if t >= 2:
                jobs.append(("wo", L, t - 2))
        if L == 1:
            jobs += [("ffnT", L, t) for t in range(NT)]
        jobs += [("up", L, c, ht) for c in range(NC) for ht in range(HT)]
        jobs += [("down", L, t) for t in range(NT)]
    return jobs


A_AT = {job: n for n, job in enumerate(ring_a_jobs())}
B_AT = {job: n for n, job in enumerate(ring_b_jobs())}


def max_items(c):
    items = []
    if c > 0:
        items += [(qt, 0, (h,), 0, CH * c) for qt in range(TPC) for h in range(G)]
    for qt in reversed(range(TPC)):
        keys = P * (qt + 1)
        per = CH // keys
        items += [(qt, 1, tuple(range(h, h + per)), CH * c, keys) for h in range(0, G, per)]
    return items


M_BANKS = 3
T_LAG = 2
LEAD = 42
TURN_AHEAD = 5
V_FIRST = 5
PV_LAG = 1
RATIO = 4.4


def attention_order():
    entries = []
    waiting = []
    for cg in range(NC * NG):
        for n, it in enumerate(max_items(cg % NC)):
            entries.append(("max", cg, it))
            if waiting and n == T_LAG:
                entries.append(("turn", waiting.pop()))
        waiting.append(cg)
    entries.append(("turn", waiting.pop()))
    order, done = [], 0

    def upto(n):
        nonlocal done
        while done < min(n, len(entries)):
            order.append(entries[done])
            done += 1

    turned = {e[1]: n + 1 for n, e in enumerate(entries) if e[0] == "turn"}
    width = 0.0
    for s, (cg, kt) in enumerate(exp_steps()):
        wide = (CH - max(kt * P - cg % NC * CH, 0)) / CH
        if kt == 0:
            upto(turned[cg] + TURN_AHEAD)
        upto(int(LEAD + RATIO * width))
        order.append(("exp", s, 0))
        upto(int(LEAD + RATIO * (width + 0.25 * wide)))
        order.append(("exp", s, 1))
        upto(int(LEAD + RATIO * (width + 0.5 * wide)))
        if s >= PV_LAG:
            order.append(("pv", s - PV_LAG))
        width += wide
    upto(len(entries))
    for s in range(len(exp_steps()) - PV_LAG, len(exp_steps())):
        order.append(("pv", s))
    return order


def exp_steps():
    return [(cg, kt) for cg in range(NC * NG) for kt in range(TPC * (cg % NC + 1))]


STEPS = exp_steps()
ORDER = attention_order()
N_MAX = sum(e[0] in ("max", "turn") for e in ORDER)
LAST_STEP = {cg: max(s for s, x in enumerate(STEPS) if x[0] == cg) for cg in range(NC * NG)}


def step_span(s):
    cg, kt = STEPS[s]
    g, c = cg // NC, cg % NC
    return g, c, kt, max(kt * P - c * CH, 0), kt * P >= c * CH


def alibi_tail():
    bf16 = mybir.dt.np(BF16)
    start = 2.0 ** -0.5
    slopes = np.array([start * start ** i for i in range(NH)], np.float32)
    bias = slopes[:, None] * (np.arange(T, dtype=np.float32) - np.float32(T - 1))[None, :]
    rest = bias.astype(np.float32) / np.float32(SCALE)
    rows = []
    for _ in range(3):
        part = rest.astype(bf16)
        rows.append(part)
        rest = rest - part.astype(np.float32)
    rows += [np.ones((NH, T), bf16)] * MAX_ROWS
    return np.stack(rows)


def two_layer_kernel(nc, a, out, tail):
    with ExitStack() as ctx:
        def sb(name, shape, dt):
            return ctx.enter_context(nc.sbuf_tensor(name, shape, dt))

        def sem(name):
            return ctx.enter_context(nc.semaphore(name))

        ps = ctx.enter_context(nc.psum_tensor("ps", [P, 8, CH], F32))
        x = sb("x", [P, NT, C], F32)
        xn = sb("xn", [P, NT, C], F32)
        xnT = sb("xnT", [P, CJ, T], F32)
        xhl = xnT[:, :, :].bitcast(FP16).rearrange("p j (s t) -> p j s t", s=2)
        parts = sb("parts", [P, 4, 3, CH], BF16)
        rest = sb("rest", [P, 2, CH], F32)
        qS = sb("qS", [P, NH, T], BF16)
        kS = sb("kS", [P, NH, T], BF16)
        v1 = sb("v1", [P, NT, NH, 2 * HD], F32)
        prob = sb("prob", [P, 3, G, CH], F32)
        oT = sb("oT", [P, NG, T], F32)
        onT = sb("onT", [P, 2, CJ, P], F32)
        rec = sb("rec", [P, 2, NH], F32)
        mx = sb("mx", [P, 2, TPC, G, 2], F32)
        mm = sb("mm", [P, 2, TPC * G], F32)
        mneg = sb("mneg", [P, 2, 2, G, TPC], BF16)
        mT = sb("mT", [2 * G * TPC, 2, P], BF16)
        w0 = sb("w0", [P, 4, CJ, C], F32)
        w1r = oT[:, :, :].rearrange("p g t -> p (g t)")[:, 0:4 * CJ * C].rearrange(
            "p (m j i) -> p m j i", m=4, j=CJ)
        w1T = sb("w1T", [P, 4, CJ, C], F32)
        bqk = sb("bqk", [P, 2, CJ], F32)
        bv = sb("bv", [P, CJ], F32)
        bo = sb("bo", [P, C], F32)
        flat = prob[:, :, :, :].rearrange("p r g q -> p (r g q)")
        g0 = flat[:, 0:2 * HT * C].rearrange("p (m k i) -> p m k i", m=2, k=HT)
        d0 = flat[:, 2 * HT * C:2 * HT * C + CJ * HID0].rearrange("p (j i) -> p j i", j=CJ)
        s0 = sb("s0", [P, 2, HT], F32)
        sd0 = sb("sd0", [P, CJ], F32)
        gu0T = sb("gu0T", [P, 2, CJ, HID0], F32)
        d0T = sb("d0T", [P, HT, C], F32)
        w8 = oT[:, :, :].rearrange("p g t -> p (g t)")[:, 0:CJ * HID1]
        w8m = oT[:, :, :].rearrange("p g t -> p (g t)")[:, CJ * HID1:2 * CJ * HID1]
        gu1 = sb("gu1", [P, 2, CJ, HID1], FP16)
        d1 = w0[:, :, :, :].rearrange("p m j i -> p (m j i)")[:, 0:HT * C].rearrange("p (k i) -> p k i", k=HT)
        s1 = sb("s1", [P, 2, HT], F32)
        sd1 = sb("sd1", [P, C], F32)
        stats = sb("stats", [P, NT, 6], F32)
        mv = sb("mv", [P, NT, 2], F32)
        ve = sb("ve", [P, NT], F32)
        rstd = sb("rstd", [P, NT], F32)
        nhalf = sb("nhalf", [P, NT], F32)
        ident = sb("ident", [P, P], F32)
        identb = sb("identb", [P, P], BF16)
        mask_q = sb("mask_q", [P, P], BF16)
        mask_k = sb("mask_k", [P, P], BF16)
        fT = qS[:, :, :].rearrange("p h t -> p (h t)").bitcast(F32)[:, 0:HT * T].rearrange(
            "p (k t) -> p k t", k=HT)
        sg = rest


        qk_dram = nc.dram_tensor("qk_scratch", [LAYERS, 2, C, len(Q_PARTS), T], BF16, kind="Internal").ap()
        m_dram = nc.dram_tensor("m_scratch", [LAYERS, NC * NG, MAX_ROWS * G * TPC, P], BF16, kind="Internal").ap()

        x_in = [sem(f"x_in{h}") for h in range(2)]
        w0_in = sem("w0_in")
        b0_in = sem("b0_in")
        w1_in = sem("w1_in")
        ffn0_in = sem("ffn0_in")
        ffn1s_in = sem("ffn1s_in")
        w8_in = sem("w8_in")
        tail_in = sem("tail_in")
        a_full, a_free = sem("a_full"), sem("a_free")
        b_full, b_free = sem("b_full"), sem("b_free")
        s_full, s_free = sem("s_full"), sem("s_free")
        m_full, m_free = sem("m_full"), sem("m_free")
        pv_done, o_taken = sem("pv_done"), sem("o_taken")
        consts, consts_step = sem("consts"), sem("consts_step")
        stats_done, rstd_done, xn_done = sem("stats_done"), sem("rstd_done"), sem("xn_done")
        rstd_step = sem("rstd_step")
        dve_step = sem("dve_step")
        hi_done, mid_done, lo_done = sem("hi_done"), sem("mid_done"), sem("lo_done")
        stacked = [sem(f"stacked{n}") for n in range(N_QK)]
        saved = [sem(f"saved{k}") for k in range(4)]
        m_saved = sem("m_saved")
        mneg_done, mT_done = sem("mneg_done"), sem("mT_done")
        m_stacked = [sem(f"m_stacked{k}") for k in range(2)]
        ones_k = sem("ones_k")
        ffn0_w, ffn0_d = sem("ffn0_w"), sem("ffn0_d")
        w8_exp, w8_round, w8_step = sem("w8_exp"), sem("w8_round"), sem("w8_step")
        bo_done = sem("bo_done")
        x_biased = sem("x_biased")
        silu_done, f_done = sem("silu_done"), sem("f_done")
        fx_hi = sem("fx_hi")
        x_final = sem("x_final")
        stored = sem("stored")

        ctx.enter_context(nc.allow_non_contiguous_dma(reason="biases and scales, a few elements per partition"))
        block = ctx.enter_context(nc.Block())

        N_STEP = len(STEPS)

        def attn_w(L, m):
            return w0[:, m] if L == 0 else w1T[:, m]

        @block.sync
        def _(sp):
            xin = a["L0_attn_x"].rearrange("o (t p) c -> p (o t) c", p=P)
            for h in range(2):
                sp.dma_start(x[:, 4 * h:4 * h + 4, :], xin[:, 4 * h:4 * h + 4, :]).then_inc(x_in[h], 16)
            sp.dma_start(kS[QK_ROWS:K_EXP[0], :, :], tail).then_inc(tail_in, 16)
            for m, n in enumerate(("Wq", "Wk", "Wv", "Wo")):
                sp.dma_start(w1r[:, m], a[f"L1_attn_{n}"].rearrange("(j p) i -> p j i", p=P)).then_inc(w1_in, 16)
            full = HID0 // P
            for m, n in enumerate(("gate", "up")):
                w = a[f"L0_ffn_wq_{n}"]
                sp.dma_start(g0[:, m, 0:full].bitcast(I32), w[0:full * P].rearrange("(k p) i -> p k i", p=P)).then_inc(ffn0_in, 16)
                sp.dma_start(g0[0:HID0 - full * P, m, full].bitcast(I32), w[full * P:HID0]).then_inc(ffn0_in, 16)
            sp.dma_start(d0[:, :, :].bitcast(I32), a["L0_ffn_wq_down"].rearrange("(j p) i -> p j i", p=P)).then_inc(ffn0_in, 16)
            def spread(L, n):
                for k in (n, n + 1):
                    mt, c, w = qk_job(k)
                    for part, done in enumerate((hi_done, mid_done, lo_done)):
                        rows = [r for r, stands in enumerate((Q_PARTS, K_PARTS)[w]) if stands == part]
                        apart = rows[1] - rows[0] if len(rows) > 1 else 1
                        sp.wait_ge(done, L * N_QK + k + 1)
                        sp.dma_start(qk_dram[L, w, mt * P:(mt + 1) * P, rows[0]:rows[-1] + 1:apart, c * CH:(c + 1) * CH],
                                     parts[:, k % 4, part].unsqueeze(1).to_broadcast([P, len(rows), CH])).then_inc(saved[k % 4], 16)
                for k in (n, n + 1):
                    mt, c, w = qk_job(k)
                    sp.wait_ge(saved[k % 4], 16 * 3 * (2 * L + k // 4 + 1))
                    src = qk_dram[L, w, mt * P:(mt + 1) * P, :, c * CH:(c + 1) * CH]
                    sp.dma_start((qS, kS)[w][0:QK_ROWS, mt * NH // CJ:(mt + 1) * NH // CJ, c * CH:(c + 1) * CH],
                                 src.rearrange("(h d) r t -> (d r) h t", d=HD)).then_inc(stacked[k], 16)

            def spread_max(L, cg):
                g, c = cg // NC, cg % NC
                n = L * NC * NG + cg
                sp.wait_ge(mT_done, n + 1)
                sp.dma_start(m_dram[L, cg], mT[:, cg % 2, :]).then_inc(m_saved, 16)
                sp.wait_ge(m_saved, 16 * (n + 1))
                dst = qS[K_MAX[L]:K_EXP[L], g * G:(g + 1) * G, c * CH:(c + 1) * CH]
                sp.dma_start(dst, m_dram[L, cg].rearrange("(s h t) q -> s h (t q)", s=MAX_ROWS, h=G)).then_inc(m_stacked[cg % 2], 16)

            for L in range(LAYERS):
                spread(L, 0)
                spread(L, 2)
                spread_max(L, 0)
                spread(L, 4)
                spread_max(L, 1)
                spread(L, 6)
                for cg in range(2, NC * NG):
                    spread_max(L, cg)
            yout = out.rearrange("o (t p) c -> p (o t) c", p=P)
            for t in range(NT):
                sp.wait_ge(x_final, t + 1)
                sp.dma_start(yout[:, t, :], x[:, t, :]).then_inc(stored, 16)
            sp.wait_ge(stored, 16 * NT)

        @block.gpsimd
        def _(pool):
            k = [0]

            def chain(ins):
                ins.then_inc(consts_step, 1)
                k[0] += 1
                pool.wait_ge(consts_step, k[0])

            nc.gpsimd.memset(nhalf[:], -0.5)
            nc.gpsimd.memset(ident[:], 0.0)
            nc.gpsimd.memset(identb[:], 0.0)
            nc.gpsimd.memset(mask_q[:], 0.0)
            chain(nc.gpsimd.memset(mask_k[:], 0.0))
            for m in (ident, identb):
                nc.gpsimd.affine_select(out=m[:], in_=m[:], compare_op=ALU.not_equal, fill=1.0, base=0,
                                        pattern=[[-1, P]], channel_multiplier=1)
            nc.gpsimd.affine_select(out=mask_q[:], in_=mask_q[:], compare_op=ALU.is_ge, fill=NEG, base=0,
                                    pattern=[[-1, P]], channel_multiplier=1)
            nc.gpsimd.affine_select(out=mask_k[:], in_=mask_k[:], compare_op=ALU.is_ge, fill=NEG, base=0,
                                    pattern=[[1, P]], channel_multiplier=-1).then_inc(consts, 1)

            def rstd_of(n):
                half = slice(4 * (n % 2), 4 * (n % 2) + 4)
                pool.wait_ge(stats_done, n + 1)
                nc.gpsimd.tensor_scalar(ve[:, half], mv[:, half, 1], EPS, None, ALU.add).then_inc(rstd_step, 1)
                pool.wait_ge(rstd_step, n + 1)
                nc.gpsimd.tensor_tensor(rstd[:, half], ve[:, half], nhalf[:, half], ALU.pow).then_inc(rstd_done, 1)

            rstd_of(0)
            rstd_of(1)
            pool.wait_ge(rstd_done, 2)
            chain(nc.gpsimd.memset(qS[QK_ROWS:QK_ROWS + ALIBI_ROWS[0], :, :], 1.0))
            nc.gpsimd.memset(v1[:, :, :, HD:2 * HD], 1.0).then_inc(consts, 1)
            pool.wait_ge(ffn0_in, 16 * 10)
            for m in range(2):
                for ht in range(HT):
                    r = hid_rows(0, ht)
                    w = g0[0:r, m, ht]
                    if m * HT + ht and (r < P or ht == 0):
                        pool.wait_ge(ffn0_w, m * HT + ht)
                    nc.gpsimd.tensor_scalar(w, w.bitcast(I32), -ZERO_POINT, s0[0:r, m, ht:ht + 1], ALU.add, ALU.mult).then_inc(ffn0_w, 1)
            pool.wait_ge(ffn0_w, 2 * HT)
            for j in range(CJ):
                nc.gpsimd.tensor_scalar(d0[:, j], d0[:, j].bitcast(I32), -ZERO_POINT, sd0[:, j:j + 1], ALU.add, ALU.mult).then_inc(ffn0_w, 1)
            pool.wait_ge(xn_done, NT)
            pool.wait_ge(bo_done, 1)
            for t in range(NT):
                nc.gpsimd.tensor_tensor(x[:, t], x[:, t], bo[:], ALU.add).then_inc(x_biased, 1)

            rstd_of(2)
            rstd_of(3)
            pool.wait_ge(b_full, B_AT["on", 0, 0] + 1)
            pool.wait_ge(rstd_done, 4)
            nc.gpsimd.memset(kS[K_MAX[1]:K_EXP[1], :, :], 1.0).then_inc(ones_k, 1)
            pool.wait_ge(ones_k, 1)
            pool.wait_ge(ffn1s_in, 16 * 3)
            pool.wait_ge(b_full, B_AT["wo", 0, NT - 1] + 1)
            w8_src = [a["L1_ffn_gate_w"].rearrange("(j p) i -> p j i", p=P),
                      a["L1_ffn_up_w"].rearrange("(j p) i -> p j i", p=P),
                      a["L1_ffn_down_w"].rearrange("(k p) i -> p k i", p=P)]
            for n in range(3):
                if n == 2:
                    rstd_of(4)
                    rstd_of(5)
                if n:
                    pool.wait_ge(w8_round, n)
                pool.dma_start(w8.rearrange("p (j i) -> p j i", j=w8_src[n].shape[1]), w8_src[n]).then_inc(w8_in, 16)
                pool.wait_ge(w8_exp, n + 1)
                chain(nc.gpsimd.tensor_scalar(w8m, w8m, 2.0 ** -6, 1.5 * 2.0 ** 20, ALU.max, ALU.mult))
                chain(nc.gpsimd.tensor_tensor(w8, w8, w8m, ALU.add))
                chain(nc.gpsimd.tensor_tensor(w8, w8, w8m, ALU.subtract))
                chain(nc.gpsimd.tensor_scalar(w8m, w8, 0.55 * 2.0 ** 120, 0.0, ALU.mult, ALU.mult))
                if n < 2:
                    dst = gu1[:, n].rearrange("p j i -> p (j i)")
                    nc.gpsimd.tensor_tensor(dst, w8, w8m, ALU.add).then_inc(w8_round, 1)
                else:
                    dst = d1[:, :, :].rearrange("p k i -> p (k i)")
                    chain(nc.gpsimd.tensor_tensor(dst, w8, w8m, ALU.add))
                    for ht in range(HT):
                        ins = nc.gpsimd.tensor_tensor(d1[:, ht], d1[:, ht], sd1[:], ALU.mult)
                    ins.then_inc(w8_round, 1)
            rstd_of(6)
            rstd_of(7)

        @block.tensor
        def _(pe):
            def take_a(job):
                n = A_AT[job]
                if n >= 4:
                    pe.wait_ge(a_free, n - 3)
                return ps[:, n % 4]

            def take_b(job):
                n = B_AT[job]
                if n >= 4:
                    pe.wait_ge(b_free, n - 3)
                return ps[:, 4 + n % 4]

            def projection_v(L, t):
                bank = take_a(("v", L, t))
                for j in range(CJ):
                    mmi = nc.tensor.matmul(bank[:, 0:C], xnT[:, j, t * P:(t + 1) * P], attn_w(L, 2)[:, j, :],
                                           start=j == 0, stop=j == CJ - 1)
                mmi.then_inc(a_full, 1)

            def ln_transposes(job, ln, L, take, full):
                for t in range(NT):
                    bank = take((job, L, t))
                    pe.wait_ge(xn_done, ln * NT + t + 1)
                    for j in range(CJ):
                        mmi = nc.tensor.transpose(bank[:, j * P:(j + 1) * P], xn[:, t, j * P:(j + 1) * P], ident[:])
                    mmi.then_inc(full, 1)

            def turn_w1(m):
                bank = take_a(("w1T", m))
                if m == 0:
                    pe.wait_ge(w1_in, 16 * 4)
                for jo in range(CJ):
                    for ji in range(CJ):
                        mmi = nc.tensor.transpose(bank[:, ji * C + jo * P:ji * C + (jo + 1) * P],
                                                  w1r[:, m, jo, ji * P:(ji + 1) * P], ident[:])
                mmi.then_inc(a_full, 1)

            def turn_gate_up(m, k):
                bank = take_a((("gateT", "upT")[m], k))
                pe.wait_ge(ffn0_w, m * HT + 2 * k + 2)
                for i in range(2):
                    r = hid_rows(0, 2 * k + i)
                    for j in range(CJ):
                        mmi = nc.tensor.transpose(bank[:, j * C + i * P:j * C + i * P + r],
                                                  g0[0:r, m, 2 * k + i, j * P:(j + 1) * P], ident[0:r, 0:r])
                mmi.then_inc(a_full, 1)

            def turn_down(k):
                bank = take_a(("downT", k))
                pe.wait_ge(ffn0_w, 2 * HT + CJ)
                for i in range(2):
                    r = hid_rows(0, 2 * k + i)
                    for j in range(CJ):
                        mmi = nc.tensor.transpose(bank[0:r, i * C + j * P:i * C + (j + 1) * P],
                                                  d0[:, j, (2 * k + i) * P:(2 * k + i) * P + r], ident[:])
                mmi.then_inc(a_full, 1)

            def side_job(L, n):
                if n < NT:
                    projection_v(L, n)
                elif L == 0 and n < NT + 4:
                    turn_w1(n - NT)
                elif L == 0 and n < NT + 4 + HT:
                    turn_gate_up((n - NT - 4) // (HT // 2), (n - NT - 4) % (HT // 2))
                elif L == 0 and n < NT + 4 + HT + HT // 2:
                    turn_down(n - NT - 4 - HT)

            def max_scores(L, n, cg, item):
                g, c = cg // NC, cg % NC
                qt, part, heads, key0, keys = item
                bank = ps[:, 4 + n % M_BANKS]
                q0 = c * CH + qt * P
                for i, h in enumerate(heads):
                    span = bank[:, i * keys:(i + 1) * keys]
                    mmi = nc.tensor.matmul(span, qS[0:K_MAX[L], g * G + h, q0:q0 + P],
                                           kS[0:K_MAX[L], g * G + h, key0:key0 + keys], start=True, stop=part == 0)
                    if part == 1:
                        mmi = nc.tensor.matmul(span[:, keys - P:keys], identb[:], mask_q[:], start=False, stop=True)
                mmi.then_inc(m_full, 1)

            def exp_scores(L, s, pair):
                g, c, kt, off, diagonal = step_span(s)
                n = 2 * (L * N_STEP + s) + pair
                if n >= 2:
                    pe.wait_ge(s_free, n - 1)
                for i in range(2):
                    h = g * G + 2 * pair + i
                    bank = ps[:, 2 * (n % 2) + i]
                    mmi = nc.tensor.matmul(bank[:, off:CH], kS[0:K_EXP[L], h, kt * P:(kt + 1) * P],
                                           qS[0:K_EXP[L], h, c * CH + off:(c + 1) * CH], start=True, stop=not diagonal)
                    if diagonal:
                        mmi = nc.tensor.matmul(bank[:, off:off + P], identb[:], mask_k[:], start=False, stop=True)
                mmi.then_inc(s_full, 1)

            def times_v(L, s):
                g, c, kt, off, _ = step_span(s)
                cg = STEPS[s][0]
                n = L * N_STEP + s
                pe.wait_ge(s_free, 2 * (n + 1))
                if kt == 0 and L * NC * NG + cg >= 1:
                    pe.wait_ge(o_taken, L * NC * NG + cg)
                bank = ps[:, 7]
                for h in range(G):
                    mmi = nc.tensor.matmul(bank[32 * h:32 * h + 32, off:CH], v1[:, kt, g * G + h, :],
                                           prob[:, n % 3, h, off:CH], start=kt == 0, stop=s == LAST_STEP[cg])
                mmi.then_inc(pv_done, 1)

            def attention(L):
                m_n = L * N_MAX
                pe.wait_ge(b_free, B_AT["on", L, 0])
                side = V_FIRST
                ready = set()
                for n_entry, entry in enumerate(ORDER):
                    if entry[0] == "max":
                        _, cg, item = entry
                        g, c = cg // NC, cg % NC
                        for n in range(N_QK):
                            mt, nc_, _w = qk_job(n)
                            if mt == g * CJ // NG and nc_ <= c and n not in ready:
                                pe.wait_ge(stacked[n], 16 * (L + 1))
                                ready.add(n)
                        if m_n - L * N_MAX >= M_BANKS or L:
                            pe.wait_ge(m_free, m_n - M_BANKS + 1)
                        max_scores(L, m_n, cg, item)
                        m_n += 1
                        if ("exp", 0, 0) in ORDER[n_entry:]:
                            side_job(L, side)
                            side += 1
                    elif entry[0] == "turn":
                        cg = entry[1]
                        pe.wait_ge(m_free, m_n - M_BANKS + 1)
                        pe.wait_ge(mneg_done, L * NC * NG + cg + 1)
                        nc.tensor.transpose(ps[0:2 * G * TPC, 4 + m_n % M_BANKS, 0:P // 2].bitcast(BF16),
                                            mneg[:, cg % 2].rearrange("p s h t -> p (s h t)"), identb[:]).then_inc(m_full, 1)
                        m_n += 1
                    elif entry[0] == "exp":
                        cg, kt = STEPS[entry[1]]
                        if entry[1:] == (0, 0):
                            pe.wait_ge(a_free, A_AT["onT", L, 0])
                        if kt == 0 and entry[2] == 0:
                            pe.wait_ge(m_stacked[cg % 2], 16 * (L * NC * NG // 2 + cg // 2 + 1))
                        exp_scores(L, entry[1], entry[2])
                    else:
                        times_v(L, entry[1])

            def out_projection(L):
                pe.wait_ge(m_free, (L + 1) * N_MAX)
                pe.wait_ge(o_taken, (L + 1) * NC * NG)
                pe.wait_ge(s_free, 2 * (L + 1) * N_STEP)
                for t in range(NT + 2):
                    if t < NT:
                        bank = take_b(("on", L, t))
                        for g in range(NG):
                            mmi = nc.tensor.transpose(bank[:, g * P:(g + 1) * P], oT[:, g, t * P:(t + 1) * P], ident[:])
                        mmi.then_inc(b_full, 1)
                    if 1 <= t <= NT:
                        bank = take_a(("onT", L, t - 1))
                        pe.wait_ge(b_free, B_AT["on", L, t - 1] + 1)
                        for j in range(CJ):
                            mmi = nc.tensor.transpose(bank[:, j * P:(j + 1) * P], xn[:, t - 1, j * P:(j + 1) * P], ident[:])
                        mmi.then_inc(a_full, 1)
                    if t >= 2:
                        bank = take_b(("wo", L, t - 2))
                        pe.wait_ge(a_free, A_AT["onT", L, t - 2] + 1)
                        for j in range(CJ):
                            mmi = nc.tensor.matmul(bank[:, 0:C], onT[:, t % 2, j], attn_w(L, 3)[:, j, :], start=j == 0, stop=j == CJ - 1)
                        mmi.then_inc(b_full, 1)

            def ffn(L):
                for c in range(NC):
                    for ht in range(HT):
                        r = hid_rows(L, ht)
                        for m, (name, take, full) in enumerate((("gate", take_a, a_full), ("up", take_b, b_full))):
                            bank = take((name, L, c, ht))
                            if L == 0 and ht == 0:
                                pe.wait_ge(a_free, A_AT["ffnT", L, (c + 1) * TPC - 1] + 1)
                            if L == 1 and ht == 0:
                                pe.wait_ge(b_free, B_AT["ffnT", L, (c + 1) * TPC - 1] + 1)
                            if L == 0:
                                for j in range(CJ):
                                    mmi = nc.tensor.matmul(bank[0:r, :], gu0T[:, m, j, ht * P:ht * P + r],
                                                           xnT[:, j, c * CH:(c + 1) * CH], start=j == 0, stop=j == CJ - 1)
                            else:
                                for j in range(CJ):
                                    for s in range(2):
                                        mmi = nc.tensor.matmul(bank[:, :], gu1[:, m, j, ht * P:(ht + 1) * P],
                                                               xhl[:, j, s, c * CH:(c + 1) * CH],
                                                               start=j + s == 0, stop=j == CJ - 1 and s == 1)
                            mmi.then_inc(full, 1)
                for t in range(NT):
                    bank = take_b(("down", L, t))
                    pe.wait_ge(f_done, (L * NC + t // TPC + 1) * HT)
                    if L == 1 and t == 0:
                        pe.wait_ge(w8_round, 3)
                    for ht in range(HT):
                        r = hid_rows(L, ht)
                        w = d0T if L == 0 else d1
                        mmi = nc.tensor.matmul(bank[:, 0:C], fT[0:r, ht, t * P:(t + 1) * P], w[0:r, ht, :],
                                               start=ht == 0, stop=ht == HT - 1)
                    mmi.then_inc(b_full, 1)

            pe.wait_ge(consts, 1)
            for L in range(LAYERS):
                ln_transposes("xnT", 2 * L, L, take_a, a_full)
                if L == 0:
                    pe.wait_ge(w0_in, 16 * 4)
                for n in range(N_QK):
                    mt, c, w = qk_job(n)
                    bank = take_b(("qk", L, n))
                    pe.wait_ge(a_free, A_AT["xnT", L, (c + 1) * TPC - 1] + 1)
                    for j in range(CJ):
                        mmi = nc.tensor.matmul(bank[:, :], attn_w(L, w)[:, j, mt * P:(mt + 1) * P],
                                               xnT[:, j, c * CH:(c + 1) * CH], start=j == 0, stop=j == CJ - 1)
                    mmi.then_inc(b_full, 1)
                if L == 0:
                    bank = take_b(("bias",))
                    pe.wait_ge(b0_in, 16 * 4)
                    for j in range(CJ):
                        mmi = nc.tensor.matmul(bank[:, 0:C], bv[:, j:j + 1].to_broadcast([P, P]), w0[:, 3, j, :],
                                               start=j == 0, stop=j == CJ - 1)
                    mmi.then_inc(b_full, 1)
                for side in range(V_FIRST):
                    side_job(L, side)
                if L == 0:
                    pe.wait_ge(consts, 2)
                    pe.wait_ge(tail_in, 16)
                else:
                    pe.wait_ge(ones_k, 1)
                attention(L)
                out_projection(L)
                ln_transposes("ffnT", 2 * L + 1, L, take_a if L == 0 else take_b, a_full if L == 0 else b_full)
                if L == 1:
                    pe.wait_ge(w8_round, 2)
                ffn(L)

        @block.scalar
        def _(act):
            for m, n in enumerate(("Wq", "Wk", "Wv", "Wo")):
                act.dma_start(w0[:, m], a[f"L0_attn_{n}"].rearrange("(j p) o -> p j o", p=P)).then_inc(w0_in, 16)
            for m, n in enumerate(("bq", "bk")):
                act.dma_start(bqk[:, m], a[f"L0_attn_{n}"].rearrange("(j p) -> p j", p=P)).then_inc(b0_in, 16)
            act.dma_start(bv[:], a["L0_attn_bv"].rearrange("(j p) -> p j", p=P)).then_inc(b0_in, 16)
            act.dma_start(bo[:], a["L0_attn_bo"].unsqueeze(0).to_broadcast([P, C])).then_inc(b0_in, 16)
            full = HID0 // P
            for m, n in enumerate(("gate", "up")):
                s = a[f"L0_ffn_s_{n}"]
                act.dma_start(s0[:, m, 0:full], s[0:full * P].rearrange("(k p) -> p k", p=P)).then_inc(ffn0_in, 16)
                act.dma_start(s0[0:HID0 - full * P, m, full:full + 1], s[full * P:HID0].unsqueeze(1)).then_inc(ffn0_in, 16)
                act.dma_start(s1[:, m], a[f"L1_ffn_{n}_scale"].rearrange("(k p) -> p k", p=P)).then_inc(ffn1s_in, 16)
            act.dma_start(sd0[:], a["L0_ffn_s_down"].rearrange("(j p) -> p j", p=P)).then_inc(ffn0_in, 16)
            act.dma_start(sd1[:], a["L1_ffn_down_scale"].unsqueeze(0).to_broadcast([P, C])).then_inc(ffn1s_in, 16)

            def bank_a(job):
                n = A_AT[job]
                act.wait_ge(a_full, n + 1)
                return ps[:, n % 4]

            def drain_transposed(job, L):
                for t in range(NT):
                    bank = bank_a((job, L, t))
                    nc.scalar.copy(xnT[:, :, t * P:(t + 1) * P], bank[:, 0:C].rearrange("p (j t) -> p j t", j=CJ)).then_inc(a_free, 1)

            def qk_parts(L):
                for n in range(N_QK + 1):
                    if n < N_QK:
                        mt, _, w = qk_job(n)
                        job = B_AT["qk", L, n]
                        act.wait_ge(b_full, job + 1)
                        if L * N_QK + n >= 4:
                            act.wait_ge(saved[n % 4], 16 * 3 * (2 * L + n // 4))
                        bias = bqk[:, w, mt:mt + 1] if L == 0 else 0.0
                        nc.scalar.activation(parts[:, n % 4, 0], ps[:, 4 + job % 4], ACT.Identity, bias=bias).then_inc(hi_done, 1)
                    if n >= 1:
                        act.wait_ge(b_free, B_AT["qk", L, n - 1] + 1)
                        nc.scalar.copy(parts[:, (n - 1) % 4, 1], rest[:, (n - 1) % 2]).then_inc(mid_done, 1)

            for L in range(LAYERS):
                drain_transposed("xnT", L)
                if L == 0:
                    act.wait_ge(b0_in, 16 * 4)
                qk_parts(L)
                if L == 0:
                    act.wait_ge(consts, 2)
                for t in range(NT):
                    bank = bank_a(("v", L, t))
                    nc.scalar.copy(v1[:, t, :, 0:HD], bank[:, 0:C].rearrange("p (h d) -> p h d", h=NH)).then_inc(a_free, 1)
                if L == 0:
                    for m in range(4):
                        bank = bank_a(("w1T", m))
                        nc.scalar.copy(w1T[:, m].rearrange("p j o -> p (j o)"), bank).then_inc(a_free, 1)
                    for m, name in enumerate(("gateT", "upT")):
                        for k in range(HT // 2):
                            bank = bank_a((name, k))
                            w = hid_rows(0, 2 * k) + hid_rows(0, 2 * k + 1)
                            nc.scalar.copy(gu0T[:, m, :, 2 * k * P:2 * k * P + w],
                                           bank.rearrange("p (j o) -> p j o", j=CJ)[:, :, 0:w]).then_inc(a_free, 1)
                    for k in range(HT // 2):
                        bank = bank_a(("downT", k))
                        r = hid_rows(0, 2 * k + 1)
                        if r == P:
                            nc.scalar.copy(d0T[:, 2 * k:2 * k + 2].rearrange("p k o -> p (k o)"), bank).then_inc(a_free, 1)
                        else:
                            nc.scalar.copy(d0T[:, 2 * k], bank[:, 0:C])
                            nc.scalar.copy(d0T[0:r, 2 * k + 1], bank[0:r, C:2 * C]).then_inc(a_free, 1)
                for s in range(N_STEP):
                    off = step_span(s)[3]
                    n = L * N_STEP + s
                    if n >= 3:
                        act.wait_ge(pv_done, n - 2)
                    for pair in range(G // 2):
                        m = 2 * n + pair
                        act.wait_ge(s_full, m + 1)
                        nc.scalar.activation(prob[:, n % 3, 2 * pair:2 * pair + 2, off:CH],
                                             ps[:, 2 * (m % 2):2 * (m % 2) + 2, off:CH], ACT.Exp, scale=SCALE).then_inc(s_free, 1)
                for t in range(NT):
                    bank = bank_a(("onT", L, t))
                    if t >= 2:
                        act.wait_ge(b_full, B_AT["wo", L, t - 2] + 1)
                    nc.scalar.copy(onT[:, t % 2].rearrange("p j q -> p (j q)"), bank[:, 0:C]).then_inc(a_free, 1)
                if L == 0:
                    drain_transposed("ffnT", L)
                else:
                    for t in range(NT):
                        job = B_AT["ffnT", L, t]
                        act.wait_ge(b_full, job + 1)
                        nc.scalar.copy(xhl[:, :, 0, t * P:(t + 1) * P],
                                       ps[:, 4 + job % 4, 0:C].rearrange("p (j t) -> p j t", j=CJ)).then_inc(fx_hi, 1)
                    act.wait_ge(ffn1s_in, 16 * 3)
                for c in range(NC):
                    for ht in range(HT):
                        r = hid_rows(L, ht)
                        n = (L * NC + c) * HT + ht
                        bank = bank_a(("gate", L, c, ht))
                        if n >= 2:
                            act.wait_ge(f_done, n - 1)
                        scale = 1.0 if L == 0 else s1[:, 0, ht:ht + 1]
                        nc.scalar.activation(sg[0:r, n % 2], bank[0:r], ACT.Silu, scale=scale).then_inc(a_free, 1)

        @block.vector
        def _(dve):
            k = [0]

            def chain(ins):
                ins.then_inc(dve_step, 1)
                k[0] += 1

            def settle():
                dve.wait_ge(dve_step, k[0])

            def bank_b(job):
                n = B_AT[job]
                dve.wait_ge(b_full, n + 1)
                return ps[:, 4 + n % 4]

            def ln_stats(t):
                chain(nc.vector.bn_stats(stats[:, t], x[:, t]))
                settle()
                ins = nc.vector.bn_aggr(mv[:, t], stats[:, t])
                if t % 4 == 3:
                    ins.then_inc(stats_done, 1)

            def ln_normalise(ln):
                for half in range(2):
                    dve.wait_ge(rstd_done, 2 * ln + half + 1)
                    dve.wait_ge(stats_done, 2 * ln + half + 1)
                    for t in range(4 * half, 4 * half + 4):
                        nc.vector.tensor_scalar(xn[:, t], x[:, t], mv[:, t, 0:1], rstd[:, t:t + 1],
                                                ALU.subtract, ALU.mult).then_inc(xn_done, 1)

            def round_w8(n):
                dve.wait_ge(w8_in, 16 * (n + 1))
                if n:
                    dve.wait_ge(w8_round, n)
                nc.vector.tensor_scalar(w8m.bitcast(I32), w8.bitcast(I32), 0x7F800000, None, ALU.bitwise_and).then_inc(w8_exp, 1)

            def add_to_x(job, L, t, last=False):
                bank = bank_b((job, L, t))
                ins = nc.vector.tensor_tensor(x[:, t], bank[:, 0:C], x[:, t], ALU.add)
                return ins

            def attention(L):
                m_n = L * N_MAX
                left = {}
                for entry in ORDER:
                    if entry[0] == "max":
                        _, cg, (qt, part, heads, key0, keys) = entry
                        slot = cg % 2
                        dve.wait_ge(m_full, m_n + 1)
                        src = ps[:, 4 + m_n % M_BANKS, 0:len(heads) * keys].rearrange("p (h k) -> p h k", h=len(heads))
                        ins = nc.vector.tensor_reduce(mx[:, slot, qt, heads[0]:heads[-1] + 1, part], src, AX_X, ALU.max)
                        ins.then_inc(m_free, 1)
                        m_n += 1
                        left[cg] = left.get(cg, len(max_items(cg % NC))) - 1
                        if left[cg] == 0:
                            negate_max(L, cg, m_n)
                    elif entry[0] == "turn":
                        n = L * NC * NG + entry[1]
                        dve.wait_ge(m_full, m_n + 1)
                        if n >= 2:
                            dve.wait_ge(m_stacked[n % 2], 16 * (n // 2))
                        nc.vector.tensor_copy(mT[:, entry[1] % 2], ps[0:2 * G * TPC, 4 + m_n % M_BANKS, 0:P // 2].bitcast(BF16)).then_inc(mT_done, 1)
                        dve.wait_ge(mT_done, n + 1)
                        nc.vector.engine_nop().then_inc(m_free, 1)
                        m_n += 1
                    elif entry[0] == "pv" and entry[1] == LAST_STEP[STEPS[entry[1]][0]]:
                        cg = STEPS[entry[1]][0]
                        if L == 1 and cg == 0:
                            dve.wait_ge(w8_round, 3)
                        dve.wait_ge(pv_done, L * N_STEP + entry[1] + 1)
                        g, c = cg // NC, cg % NC
                        nc.vector.tensor_copy(oT[:, g, c * CH:(c + 1) * CH], ps[:, 7]).then_inc(o_taken, 1)

            def negate_max(L, cg, m_n):
                slot = cg % 2
                dve.wait_ge(m_free, m_n)
                both = mx[:, slot].rearrange("p t h s -> p (t h) s")
                if cg % NC:
                    chain(nc.vector.tensor_tensor(mm[:, slot], both[:, :, 0], both[:, :, 1], ALU.max))
                    settle()
                    top = mm[:, slot].rearrange("p (t h) -> p h t", h=G)
                else:
                    top = both[:, :, 1].rearrange("p (t h) -> p h t", h=G)
                chain(nc.vector.tensor_scalar(mneg[:, slot, 0], top, -1.0, None, ALU.mult))
                settle()
                nc.vector.scalar_tensor_tensor(mneg[:, slot, 1], top, -1.0, mneg[:, slot, 0],
                                               ALU.mult, ALU.subtract).then_inc(mneg_done, 1)

            for h in range(2):
                dve.wait_ge(x_in[h], 16)
                for t in range(4 * h, 4 * h + 4):
                    ln_stats(t)
            for L in range(LAYERS):
                ln_normalise(2 * L)
                if L == 0:
                    dve.wait_ge(b0_in, 16 * 4)
                for n in range(N_QK + 1):
                    if n < N_QK:
                        mt, _, w = qk_job(n)
                        bank = bank_b(("qk", L, n))
                        dve.wait_ge(hi_done, L * N_QK + n + 1)
                        if L * N_QK + n >= 2:
                            dve.wait_ge(lo_done, L * N_QK + n - 1)
                        bias = bqk[:, w, mt:mt + 1] if L == 0 else 0.0
                        nc.vector.scalar_tensor_tensor(rest[:, n % 2], bank, bias, parts[:, n % 4, 0],
                                                       ALU.add, ALU.subtract).then_inc(b_free, 1)
                    if n >= 1:
                        m = n - 1
                        dve.wait_ge(mid_done, L * N_QK + m + 1)
                        nc.vector.tensor_tensor(parts[:, m % 4, 2], rest[:, m % 2], parts[:, m % 4, 1], ALU.subtract).then_inc(lo_done, 1)
                if L == 0:
                    bank = bank_b(("bias",))
                    nc.vector.tensor_tensor(bo[:], bank[:, 0:C], bo[:], ALU.add).then_inc(bo_done, 1)
                    dve.wait_ge(bo_done, 1)
                    nc.vector.engine_nop().then_inc(b_free, 1)
                if L == 1:
                    round_w8(2)
                attention(L)
                if L == 0:
                    dve.wait_ge(x_biased, NT)
                for t in range(NT + 2):
                    if t < NT:
                        bank = bank_b(("on", L, t)).rearrange("p (h d) -> p h d", h=NH)
                        chain(nc.vector.reciprocal(rec[:, t % 2].unsqueeze(2), bank[:, :, HD:HD + 1]))
                        settle()
                        nc.vector.tensor_tensor(xn[:, t].rearrange("p (h d) -> p h d", h=NH), bank[:, :, 0:HD],
                                                rec[:, t % 2].unsqueeze(2).to_broadcast([P, NH, HD]), ALU.mult).then_inc(b_free, 1)
                    if t >= 2:
                        add_to_x("wo", L, t - 2).then_inc(b_free, 1)
                        dve.wait_ge(b_free, B_AT["wo", L, t - 2] + 1)
                        ln_stats(t - 2)
                ln_normalise(2 * L + 1)
                if L == 1:
                    for t in range(NT):
                        bank = bank_b(("ffnT", L, t))[:, 0:C].rearrange("p (j t) -> p j t", j=CJ)
                        dve.wait_ge(fx_hi, t + 1)
                        nc.vector.tensor_tensor(xhl[:, :, 1, t * P:(t + 1) * P], bank, xhl[:, :, 0, t * P:(t + 1) * P],
                                                ALU.subtract).then_inc(b_free, 1)
                for c in range(NC):
                    for ht in range(HT):
                        if L == 0 and ht == 3:
                            round_w8(c)
                        r = hid_rows(L, ht)
                        n = (L * NC + c) * HT + ht
                        bank = bank_b(("up", L, c, ht))
                        dve.wait_ge(a_free, A_AT["gate", L, c, ht] + 1)
                        f = fT[0:r, ht, c * CH:(c + 1) * CH]
                        if L == 0:
                            ins = nc.vector.tensor_tensor(f, bank[0:r], sg[0:r, n % 2], ALU.mult)
                        else:
                            ins = nc.vector.scalar_tensor_tensor(f, bank[0:r], s1[:, 1, ht:ht + 1], sg[:, n % 2], ALU.mult, ALU.mult)
                        ins.then_inc(f_done, 1)
                        dve.wait_ge(f_done, n + 1)
                        nc.vector.engine_nop().then_inc(b_free, 1)
                for t in range(NT):
                    ins = add_to_x("down", L, t)
                    if L == 0:
                        ins.then_inc(b_free, 1)
                        dve.wait_ge(b_free, B_AT["down", L, t] + 1)
                        ln_stats(t)
                    else:
                        ins.then_inc(x_final, 1)
                        if t < NT - 4:
                            dve.wait_ge(x_final, t + 1)
                            nc.vector.engine_nop().then_inc(b_free, 1)


_INS = ["L0_attn_x", "L0_attn_Wq", "L0_attn_bq", "L0_attn_Wk", "L0_attn_bk", "L0_attn_Wv", "L0_attn_bv", "L0_attn_Wo",
        "L0_attn_bo", "L0_ffn_wq_gate", "L0_ffn_s_gate", "L0_ffn_wq_up", "L0_ffn_s_up", "L0_ffn_wq_down",
        "L0_ffn_s_down", "L1_attn_Wq", "L1_attn_Wk", "L1_attn_Wv", "L1_attn_Wo", "L1_ffn_gate_w", "L1_ffn_up_w",
        "L1_ffn_down_w", "L1_ffn_gate_scale", "L1_ffn_up_scale", "L1_ffn_down_scale"]


def kernel(**inputs):
    import concourse.bacc as bacc
    from concourse.bass_utils import run_bass_kernel_spmd

    nc = bacc.Bacc("TRN2", target_bir_lowering=False, num_devices=1)
    arrays, aps = {}, {}
    for name in _INS:
        arr = np.ascontiguousarray(inputs[name])
        arrays[f"in_{name}"] = arr
        aps[name] = nc.dram_tensor(f"in_{name}", arr.shape, mybir.dt.from_np(arr.dtype), kind="ExternalInput").ap()
    arrays["alibi_tail"] = alibi_tail()
    tail = nc.dram_tensor("alibi_tail", arrays["alibi_tail"].shape, BF16, kind="ExternalInput").ap()
    out = nc.dram_tensor("out", (1, T, C), F32, kind="ExternalOutput").ap()
    two_layer_kernel(nc, aps, out, tail)
    r = run_bass_kernel_spmd(nc, [arrays], core_ids=[0])
    return r.results[0]["out"]
```

```python
from contextlib import ExitStack

import numpy as np

import concourse.bass as bass
from concourse import mybir

P = 128
T, C = 1024, 256
NH, HD = 16, 16
HID0, HID1 = 704, 768
NT = T // P
CH = 512
NC = T // CH
CJ = C // P
G = 4
NG = NH // G
TPC = CH // P
LAYERS = 2
HT = 6
NEG = -3.0e38
EPS = 1e-5
ZERO_POINT = 128.0
SCALE = float(HD) ** -0.5

F32, BF16, FP16, I32 = mybir.dt.float32, mybir.dt.bfloat16, mybir.dt.float16, mybir.dt.int32
ALU = mybir.AluOpType
ACT = mybir.ActivationFunctionType
AX_X = mybir.AxisListType.X

Q_PARTS = (0, 0, 0, 1, 1, 2)
K_PARTS = (2, 0, 1, 0, 1, 0)
QK_ROWS = len(Q_PARTS) * HD
ALIBI_ROWS = (3, 0)
MAX_ROWS = 2
K_MAX = [QK_ROWS + a for a in ALIBI_ROWS]
K_EXP = [k + MAX_ROWS for k in K_MAX]


def qk_job(n):
    return n // (2 * NC), n // 2 % NC, n % 2


N_QK = CJ * NC * 2


def hid_rows(layer, ht):
    return min(P, (HID0, HID1)[layer] - ht * P)



def ring_a_jobs():
    jobs = []
    for L in range(LAYERS):
        jobs += [("xnT", L, t) for t in range(NT)]
        jobs += [("v", L, t) for t in range(NT)]
        if L == 0:
            jobs += [("w1T", m) for m in range(4)]
            jobs += [(w, k) for w in ("gateT", "upT", "downT") for k in range(HT // 2)]
        jobs += [("onT", L, t) for t in range(NT)]
        gates = [("gate", L, c, ht) for c in range(NC) for ht in range(HT)]
        turns = [("ffnT", L, t) for t in range(NT)] if L == 0 else []
        jobs += turns[0:TPC] + gates[0:1] + turns[TPC:] + gates[1:]
    return jobs


def ring_b_jobs():
    jobs = []
    for L in range(LAYERS):
        jobs += [("qk", L, n) for n in range(N_QK)]
        if L == 0:
            jobs.append(("bias",))
        for t in range(NT + 2):
            if t < NT:
                jobs.append(("on", L, t))
            if t >= 2:
                jobs.append(("wo", L, t - 2))
        ups = [("up", L, c, ht) for c in range(NC) for ht in range(HT)]
        turns = [("ffnT", L, t) for t in range(NT)] if L == 1 else []
        jobs += turns[0:TPC] + ups[0:1] + turns[TPC:] + ups[1:]
        jobs += [("down", L, t) for t in range(NT)]
    return jobs


A_AT = {job: n for n, job in enumerate(ring_a_jobs())}
B_AT = {job: n for n, job in enumerate(ring_b_jobs())}


def max_items(c):
    items = []
    if c > 0:
        items += [(qt, 0, (h,), 0, CH * c) for qt in range(TPC) for h in range(G)]
    for qt in reversed(range(TPC)):
        keys = P * (qt + 1)
        per = CH // keys
        items += [(qt, 1, tuple(range(h, h + per)), CH * c, keys) for h in range(0, G, per)]
    return items


M_BANKS = 3
T_LAG = 2
LEAD = 42
TURN_AHEAD = 5
FIRST_HALF_AFTER = 5
QK_FIRST = 1
V_FIRST = 5
PV_LAG = 1
RATIO = 4.4


def attention_order():
    entries = []
    waiting = []
    for cg in range(NC * NG):
        for n, it in enumerate(max_items(cg % NC)):
            entries.append(("max", cg, it))
            if waiting and n == T_LAG:
                entries.append(("turn", waiting.pop()))
        waiting.append(cg)
    entries.append(("turn", waiting.pop()))
    order, done = [], 0

    def upto(n):
        nonlocal done
        while done < min(n, len(entries)):
            order.append(entries[done])
            done += 1

    turned = {e[1]: n + 1 for n, e in enumerate(entries) if e[0] == "turn"}
    width = 0.0
    for s, (cg, kt) in enumerate(exp_steps()):
        wide = (CH - max(kt * P - cg % NC * CH, 0)) / CH
        if kt == 0:
            upto(turned[cg] + TURN_AHEAD)
        upto(int(LEAD + RATIO * width))
        order.append(("exp", s, 0))
        upto(int(LEAD + RATIO * (width + 0.25 * wide)))
        order.append(("exp", s, 1))
        upto(int(LEAD + RATIO * (width + 0.5 * wide)))
        if s >= PV_LAG:
            order.append(("pv", s - PV_LAG))
        width += wide
    upto(len(entries))
    for s in range(len(exp_steps()) - PV_LAG, len(exp_steps())):
        order.append(("pv", s))
    return order


def exp_steps():
    return [(cg, kt) for cg in range(NC * NG) for kt in range(TPC * (cg % NC + 1))]


STEPS = exp_steps()
ORDER = attention_order()
N_MAX = sum(e[0] in ("max", "turn") for e in ORDER)
LAST_STEP = {cg: max(s for s, x in enumerate(STEPS) if x[0] == cg) for cg in range(NC * NG)}


def step_span(s):
    cg, kt = STEPS[s]
    g, c = cg // NC, cg % NC
    return g, c, kt, max(kt * P - c * CH, 0), kt * P >= c * CH


def alibi_tail():
    bf16 = mybir.dt.np(BF16)
    start = 2.0 ** -0.5
    slopes = np.array([start * start ** i for i in range(NH)], np.float32)
    bias = slopes[:, None] * (np.arange(T, dtype=np.float32) - np.float32(T - 1))[None, :]
    rest = bias.astype(np.float32) / np.float32(SCALE)
    rows = []
    for _ in range(3):
        part = rest.astype(bf16)
        rows.append(part)
        rest = rest - part.astype(np.float32)
    rows += [np.ones((NH, T), bf16)] * MAX_ROWS
    return np.stack(rows)


def two_layer_kernel(nc, a, out, tail):
    with ExitStack() as ctx:
        def sb(name, shape, dt):
            return ctx.enter_context(nc.sbuf_tensor(name, shape, dt))

        def sem(name):
            return ctx.enter_context(nc.semaphore(name))

        ps = ctx.enter_context(nc.psum_tensor("ps", [P, 8, CH], F32))
        x = sb("x", [P, NT, C], F32)
        xn = sb("xn", [P, NT, C], F32)
        xnT = sb("xnT", [P, CJ, T], F32)
        xhl = xnT[:, :, :].bitcast(FP16).rearrange("p j (s t) -> p j s t", s=2)
        parts = sb("parts", [P, 4, 3, CH], BF16)
        rest = sb("rest", [P, 2, CH], F32)
        qS = sb("qS", [P, NH, T], BF16)
        kS = sb("kS", [P, NH, T], BF16)
        v1 = sb("v1", [P, NT, NH, 2 * HD], F32)
        prob = sb("prob", [P, 3, G, CH], F32)
        oT = sb("oT", [P, NG, T], F32)
        onT = sb("onT", [P, 2, CJ, P], F32)
        rec = sb("rec", [P, 2, NH], F32)
        mx = sb("mx", [P, 2, TPC, G, 2], F32)
        mm = sb("mm", [P, 2, TPC * G], F32)
        mneg = sb("mneg", [P, 2, 2, G, TPC], BF16)
        mT = sb("mT", [2 * G * TPC, 2, P], BF16)
        w0 = sb("w0", [P, 4, CJ, C], F32)
        w1r = oT[:, :, :].rearrange("p g t -> p (g t)")[:, 0:4 * CJ * C].rearrange(
            "p (m j i) -> p m j i", m=4, j=CJ)
        w1T = sb("w1T", [P, 4, CJ, C], F32)
        bqk = sb("bqk", [P, 2, CJ], F32)
        bv = sb("bv", [P, CJ], F32)
        bo = sb("bo", [P, C], F32)
        flat = prob[:, :, :, :].rearrange("p r g q -> p (r g q)")
        g0 = flat[:, 0:2 * HT * C].rearrange("p (m k i) -> p m k i", m=2, k=HT)
        d0 = flat[:, 2 * HT * C:2 * HT * C + CJ * HID0].rearrange("p (j i) -> p j i", j=CJ)
        s0 = sb("s0", [P, 2, HT], F32)
        sd0 = sb("sd0", [P, CJ], F32)
        gu0T = sb("gu0T", [P, 2, CJ, HID0], F32)
        d0T = sb("d0T", [P, HT, C], F32)
        w8 = oT[:, :, :].rearrange("p g t -> p (g t)")[:, 0:CJ * HID1]
        w8m = oT[:, :, :].rearrange("p g t -> p (g t)")[:, CJ * HID1:2 * CJ * HID1]
        gu1 = sb("gu1", [P, 2, CJ, HID1], FP16)
        d1 = w0[:, :, :, :].rearrange("p m j i -> p (m j i)").bitcast(BF16)[:, 0:HT * C].rearrange("p (k i) -> p k i", k=HT)
        s1 = sb("s1", [P, 2, HT], F32)
        sd1 = sb("sd1", [P, C], F32)
        stats = sb("stats", [P, NT, 6], F32)
        mv = sb("mv", [P, NT, 2], F32)
        ve = sb("ve", [P, NT], F32)
        rstd = sb("rstd", [P, NT], F32)
        nhalf = sb("nhalf", [P, NT], F32)
        ident = sb("ident", [P, P], F32)
        identb = sb("identb", [P, P], BF16)
        mask_q = sb("mask_q", [P, P], BF16)
        mask_k = sb("mask_k", [P, P], BF16)
        fT = qS[:, :, :].rearrange("p h t -> p (h t)").bitcast(F32)[:, 0:HT * T].rearrange(
            "p (k t) -> p k t", k=HT)
        f3 = [qS[:, 0:HT], qS[:, HT:2 * HT], kS[:, 0:HT]]
        f_whole, f_rest = prob[:, :, 0], prob[:, :, 1]
        y = prob[:, :, 2, 0:C]
        sg = rest

        qk_dram = nc.dram_tensor("qk_scratch", [LAYERS, 2, C, len(Q_PARTS), T], BF16, kind="Internal").ap()
        m_dram = nc.dram_tensor("m_scratch", [LAYERS, NC * NG, MAX_ROWS * G * TPC, P], BF16, kind="Internal").ap()

        x_in = [sem(f"x_in{h}") for h in range(2)]
        w0_in, wvo_in = sem("w0_in"), sem("wvo_in")
        b0_in, bvo_in = sem("b0_in"), sem("bvo_in")
        w1_in = sem("w1_in")
        ffn0_in = sem("ffn0_in")
        ffn1s_in = sem("ffn1s_in")
        w8_in = sem("w8_in")
        tail_in = sem("tail_in")
        a_full, a_free = sem("a_full"), sem("a_free")
        b_full, b_free = sem("b_full"), sem("b_free")
        s_full, s_free = sem("s_full"), sem("s_free")
        m_full, m_free = sem("m_full"), sem("m_free")
        pv_done, o_taken = sem("pv_done"), sem("o_taken")
        consts, consts_step = sem("consts"), sem("consts_step")
        stats_done, rstd_done, xn_done = sem("stats_done"), sem("rstd_done"), sem("xn_done")
        rstd_step = sem("rstd_step")
        dve_step = sem("dve_step")
        hi_done, mid_done, lo_done = sem("hi_done"), sem("mid_done"), sem("lo_done")
        stacked = [sem(f"stacked{n}") for n in range(N_QK)]
        saved = [sem(f"saved{k}") for k in range(4)]
        m_saved = sem("m_saved")
        mneg_done, mT_done = sem("mneg_done"), sem("mT_done")
        m_stacked = [sem(f"m_stacked{k}") for k in range(2)]
        ones_k = sem("ones_k")
        ffn0_w = sem("ffn0_w")
        w8_exp, w8_round = sem("w8_exp"), sem("w8_round")
        bo_done = sem("bo_done")
        x_biased = sem("x_biased")
        f_done = sem("f_done")
        fx_hi = sem("fx_hi")
        f_hi, f_left, f_mid, f_lo = sem("f_hi"), sem("f_left"), sem("f_mid"), sem("f_lo")
        y_done = sem("y_done")
        x_final = sem("x_final")
        stored = sem("stored")

        ctx.enter_context(nc.allow_non_contiguous_dma(reason="biases and scales, a few elements per partition"))
        block = ctx.enter_context(nc.Block())

        N_STEP = len(STEPS)

        def attn_w(L, m):
            return w0[:, m] if L == 0 else w1T[:, m]

        @block.sync
        def _(sp):
            xin = a["L0_attn_x"].rearrange("o (t p) c -> p (o t) c", p=P)
            for h in range(2):
                sp.dma_start(x[:, 4 * h:4 * h + 4, :], xin[:, 4 * h:4 * h + 4, :]).then_inc(x_in[h], 16)
            for m, n in ((2, "Wv"), (3, "Wo")):
                sp.dma_start(w0[:, m], a[f"L0_attn_{n}"].rearrange("(j p) o -> p j o", p=P)).then_inc(wvo_in, 16)
            sp.dma_start(bv[:], a["L0_attn_bv"].rearrange("(j p) -> p j", p=P)).then_inc(bvo_in, 16)
            sp.dma_start(bo[:], a["L0_attn_bo"].unsqueeze(0).to_broadcast([P, C])).then_inc(bvo_in, 16)
            full = HID0 // P
            for m, n in enumerate(("gate", "up")):
                s = a[f"L0_ffn_s_{n}"]
                sp.dma_start(s0[:, m, 0:full], s[0:full * P].rearrange("(k p) -> p k", p=P)).then_inc(ffn0_in, 16)
                sp.dma_start(s0[0:HID0 - full * P, m, full:full + 1], s[full * P:HID0].unsqueeze(1)).then_inc(ffn0_in, 16)
                w = a[f"L0_ffn_wq_{n}"]
                sp.dma_start(g0[:, m, 0:full].bitcast(I32), w[0:full * P].rearrange("(k p) i -> p k i", p=P)).then_inc(ffn0_in, 16)
                sp.dma_start(g0[0:HID0 - full * P, m, full].bitcast(I32), w[full * P:HID0]).then_inc(ffn0_in, 16)
            sp.dma_start(sd0[:], a["L0_ffn_s_down"].rearrange("(j p) -> p j", p=P)).then_inc(ffn0_in, 16)
            sp.dma_start(d0[:, :, :].bitcast(I32), a["L0_ffn_wq_down"].rearrange("(j p) i -> p j i", p=P)).then_inc(ffn0_in, 16)
            sp.dma_start(kS[QK_ROWS:K_EXP[0], :, :], tail).then_inc(tail_in, 16)
            for m, n in enumerate(("Wq", "Wk", "Wv", "Wo")):
                sp.dma_start(w1r[:, m], a[f"L1_attn_{n}"].rearrange("(j p) i -> p j i", p=P)).then_inc(w1_in, 16)

            def save(L, k):
                mt, c, w = qk_job(k)
                for part, done in enumerate((hi_done, mid_done, lo_done)):
                    rows = [r for r, stands in enumerate((Q_PARTS, K_PARTS)[w]) if stands == part]
                    apart = rows[1] - rows[0] if len(rows) > 1 else 1
                    sp.wait_ge(done, L * N_QK + k + 1)
                    sp.dma_start(qk_dram[L, w, mt * P:(mt + 1) * P, rows[0]:rows[-1] + 1:apart, c * CH:(c + 1) * CH],
                                 parts[:, k % 4, part].unsqueeze(1).to_broadcast([P, len(rows), CH])).then_inc(saved[k % 4], 16)

            def spread(L, k):
                mt, c, w = qk_job(k)
                sp.wait_ge(saved[k % 4], 16 * 3 * (2 * L + k // 4 + 1))
                src = qk_dram[L, w, mt * P:(mt + 1) * P, :, c * CH:(c + 1) * CH]
                sp.dma_start((qS, kS)[w][0:QK_ROWS, mt * NH // CJ:(mt + 1) * NH // CJ, c * CH:(c + 1) * CH],
                             src.rearrange("(h d) r t -> (d r) h t", d=HD)).then_inc(stacked[k], 16)

            def spread_max(L, cg):
                g, c = cg // NC, cg % NC
                n = L * NC * NG + cg
                sp.wait_ge(mT_done, n + 1)
                sp.dma_start(m_dram[L, cg], mT[:, cg % 2, :]).then_inc(m_saved, 16)
                sp.wait_ge(m_saved, 16 * (n + 1))
                dst = qS[K_MAX[L]:K_EXP[L], g * G:(g + 1) * G, c * CH:(c + 1) * CH]
                sp.dma_start(dst, m_dram[L, cg].rearrange("(s h t) q -> s h (t q)", s=MAX_ROWS, h=G)).then_inc(m_stacked[cg % 2], 16)

            for L in range(LAYERS):
                for k in range(0, 4):
                    save(L, k)
                for k in range(0, N_QK - 4, 2):
                    spread(L, k)
                    spread(L, k + 1)
                    save(L, k + 4)
                    save(L, k + 5)
                for k in range(N_QK - 4, N_QK):
                    spread(L, k)
                if L == 0:
                    for m, n in enumerate(("gate", "up")):
                        sp.dma_start(s1[:, m], a[f"L1_ffn_{n}_scale"].rearrange("(k p) -> p k", p=P)).then_inc(ffn1s_in, 16)
                    sp.dma_start(sd1[:], a["L1_ffn_down_scale"].unsqueeze(0).to_broadcast([P, C])).then_inc(ffn1s_in, 16)
                for cg in range(NC * NG):
                    spread_max(L, cg)
            yout = out.rearrange("o (t p) c -> p (o t) c", p=P)
            for t in range(NT):
                sp.wait_ge(x_final, t + 1)
                sp.dma_start(yout[:, t, :], x[:, t, :]).then_inc(stored, 16)
            sp.wait_ge(stored, 16 * NT)

        @block.gpsimd
        def _(pool):
            k = [0]

            def chain(ins):
                ins.then_inc(consts_step, 1)
                k[0] += 1
                pool.wait_ge(consts_step, k[0])

            nc.gpsimd.memset(nhalf[:], -0.5)
            nc.gpsimd.memset(ident[:], 0.0)
            nc.gpsimd.memset(identb[:], 0.0)
            nc.gpsimd.memset(mask_q[:], 0.0)
            chain(nc.gpsimd.memset(mask_k[:], 0.0))
            for m in (ident, identb):
                nc.gpsimd.affine_select(out=m[:], in_=m[:], compare_op=ALU.not_equal, fill=1.0, base=0,
                                        pattern=[[-1, P]], channel_multiplier=1)
            nc.gpsimd.affine_select(out=mask_q[:], in_=mask_q[:], compare_op=ALU.is_ge, fill=NEG, base=0,
                                    pattern=[[-1, P]], channel_multiplier=1)
            nc.gpsimd.affine_select(out=mask_k[:], in_=mask_k[:], compare_op=ALU.is_ge, fill=NEG, base=0,
                                    pattern=[[1, P]], channel_multiplier=-1).then_inc(consts, 1)

            def rstd_of(n):
                half = slice(4 * (n % 2), 4 * (n % 2) + 4)
                pool.wait_ge(stats_done, n + 1)
                nc.gpsimd.tensor_scalar(ve[:, half], mv[:, half, 1], EPS, None, ALU.add).then_inc(rstd_step, 1)
                pool.wait_ge(rstd_step, n + 1)
                nc.gpsimd.tensor_tensor(rstd[:, half], ve[:, half], nhalf[:, half], ALU.pow).then_inc(rstd_done, 1)

            rstd_of(0)
            rstd_of(1)
            pool.wait_ge(rstd_done, 2)
            chain(nc.gpsimd.memset(qS[QK_ROWS:QK_ROWS + ALIBI_ROWS[0], :, :], 1.0))
            nc.gpsimd.memset(v1[:, :, :, HD:2 * HD], 1.0).then_inc(consts, 1)
            pool.wait_ge(ffn0_in, 16 * 10)
            for m in range(2):
                for ht in range(HT):
                    r = hid_rows(0, ht)
                    w = g0[0:r, m, ht]
                    if m * HT + ht and (r < P or ht == 0):
                        pool.wait_ge(ffn0_w, m * HT + ht)
                    nc.gpsimd.tensor_scalar(w, w.bitcast(I32), -ZERO_POINT, s0[0:r, m, ht:ht + 1], ALU.add, ALU.mult).then_inc(ffn0_w, 1)
            pool.wait_ge(ffn0_w, 2 * HT)
            for j in range(CJ):
                nc.gpsimd.tensor_scalar(d0[:, j], d0[:, j].bitcast(I32), -ZERO_POINT, sd0[:, j:j + 1], ALU.add, ALU.mult).then_inc(ffn0_w, 1)
            pool.wait_ge(xn_done, NT)
            pool.wait_ge(bo_done, 1)
            for t in range(NT):
                nc.gpsimd.tensor_tensor(x[:, t], x[:, t], bo[:], ALU.add).then_inc(x_biased, 1)

            rstd_of(2)
            rstd_of(3)
            pool.wait_ge(ffn1s_in, 16 * 3)
            pool.wait_ge(b_full, B_AT["wo", 0, NT - 1] + 1)
            w8_src = [a["L1_ffn_gate_w"].rearrange("(j p) i -> p j i", p=P),
                      a["L1_ffn_up_w"].rearrange("(j p) i -> p j i", p=P),
                      a["L1_ffn_down_w"].rearrange("(k p) i -> p k i", p=P)]
            for n in range(3):
                if n == 2:
                    rstd_of(4)
                    rstd_of(5)
                if n:
                    pool.wait_ge(w8_round, n)
                pool.dma_start(w8.rearrange("p (j i) -> p j i", j=w8_src[n].shape[1]), w8_src[n]).then_inc(w8_in, 16)
                if n == 0:
                    pool.wait_ge(rstd_done, 4)
                    nc.gpsimd.memset(kS[K_MAX[1]:K_EXP[1], :, :], 1.0).then_inc(ones_k, 1)
                    pool.wait_ge(ones_k, 1)
                pool.wait_ge(w8_exp, n + 1)
                chain(nc.gpsimd.tensor_scalar(w8m, w8m, 2.0 ** -6, 1.5 * 2.0 ** 20, ALU.max, ALU.mult))
                chain(nc.gpsimd.tensor_tensor(w8, w8, w8m, ALU.add))
                chain(nc.gpsimd.tensor_tensor(w8, w8, w8m, ALU.subtract))
                chain(nc.gpsimd.tensor_scalar(w8m, w8, 0.55 * 2.0 ** 120, 0.0, ALU.mult, ALU.mult))
                if n < 2:
                    dst = gu1[:, n].rearrange("p j i -> p (j i)")
                    nc.gpsimd.tensor_tensor(dst, w8, w8m, ALU.add).then_inc(w8_round, 1)
                else:
                    dst = d1[:, :, :].rearrange("p k i -> p (k i)")
                    nc.gpsimd.tensor_tensor(dst, w8, w8m, ALU.add).then_inc(w8_round, 1)
            rstd_of(6)
            rstd_of(7)
            for n in range(NC * HT):
                span = slice(n // HT * CH, (n // HT + 1) * CH)
                pool.wait_ge(f_left, n + 1)
                pool.wait_ge(f_mid, n + 1)
                nc.gpsimd.tensor_tensor(f3[2][:, n % HT, span], f_rest[:, n % 3], f3[1][:, n % HT, span], ALU.subtract).then_inc(f_lo, 1)

        @block.tensor
        def _(pe):
            def take_a(job):
                n = A_AT[job]
                if n >= 4:
                    pe.wait_ge(a_free, n - 3)
                return ps[:, n % 4]

            def take_b(job):
                n = B_AT[job]
                if n >= 4:
                    pe.wait_ge(b_free, n - 3)
                return ps[:, 4 + n % 4]

            def projection_v(L, t):
                bank = take_a(("v", L, t))
                for j in range(CJ):
                    mmi = nc.tensor.matmul(bank[:, 0:C], xnT[:, j, t * P:(t + 1) * P], attn_w(L, 2)[:, j, :],
                                           start=j == 0, stop=j == CJ - 1)
                mmi.then_inc(a_full, 1)

            def ln_transposes(job, ln, half, L, take, full):
                for t in range(TPC * half, TPC * (half + 1)):
                    bank = take((job, L, t))
                    pe.wait_ge(xn_done, ln * NT + t + 1)
                    for j in range(CJ):
                        mmi = nc.tensor.transpose(bank[:, j * P:(j + 1) * P], xn[:, t, j * P:(j + 1) * P], ident[:])
                    mmi.then_inc(full, 1)

            def turn_w1(m):
                bank = take_a(("w1T", m))
                if m == 0:
                    pe.wait_ge(w1_in, 16 * 4)
                for jo in range(CJ):
                    for ji in range(CJ):
                        mmi = nc.tensor.transpose(bank[:, ji * C + jo * P:ji * C + (jo + 1) * P],
                                                  w1r[:, m, jo, ji * P:(ji + 1) * P], ident[:])
                mmi.then_inc(a_full, 1)

            def turn_gate_up(m, k):
                bank = take_a((("gateT", "upT")[m], k))
                pe.wait_ge(ffn0_w, m * HT + 2 * k + 2)
                for i in range(2):
                    r = hid_rows(0, 2 * k + i)
                    for j in range(CJ):
                        mmi = nc.tensor.transpose(bank[:, j * C + i * P:j * C + i * P + r],
                                                  g0[0:r, m, 2 * k + i, j * P:(j + 1) * P], ident[0:r, 0:r])
                mmi.then_inc(a_full, 1)

            def turn_down(k):
                bank = take_a(("downT", k))
                pe.wait_ge(ffn0_w, 2 * HT + CJ)
                for i in range(2):
                    r = hid_rows(0, 2 * k + i)
                    for j in range(CJ):
                        mmi = nc.tensor.transpose(bank[0:r, i * C + j * P:i * C + (j + 1) * P],
                                                  d0[:, j, (2 * k + i) * P:(2 * k + i) * P + r], ident[:])
                mmi.then_inc(a_full, 1)

            def side_job(L, n):
                if n < NT:
                    projection_v(L, n)
                elif L == 0 and n < NT + 4:
                    turn_w1(n - NT)
                elif L == 0 and n < NT + 4 + HT:
                    turn_gate_up((n - NT - 4) // (HT // 2), (n - NT - 4) % (HT // 2))
                elif L == 0 and n < NT + 4 + HT + HT // 2:
                    turn_down(n - NT - 4 - HT)

            def max_scores(L, n, cg, item):
                g, c = cg // NC, cg % NC
                qt, part, heads, key0, keys = item
                bank = ps[:, 4 + n % M_BANKS]
                q0 = c * CH + qt * P
                for i, h in enumerate(heads):
                    span = bank[:, i * keys:(i + 1) * keys]
                    mmi = nc.tensor.matmul(span, qS[0:K_MAX[L], g * G + h, q0:q0 + P],
                                           kS[0:K_MAX[L], g * G + h, key0:key0 + keys], start=True, stop=part == 0)
                    if part == 1:
                        mmi = nc.tensor.matmul(span[:, keys - P:keys], identb[:], mask_q[:], start=False, stop=True)
                mmi.then_inc(m_full, 1)

            def exp_scores(L, s, pair):
                g, c, kt, off, diagonal = step_span(s)
                n = 2 * (L * N_STEP + s) + pair
                if n >= 2:
                    pe.wait_ge(s_free, n - 1)
                for i in range(2):
                    h = g * G + 2 * pair + i
                    bank = ps[:, 2 * (n % 2) + i]
                    mmi = nc.tensor.matmul(bank[:, off:CH], kS[0:K_EXP[L], h, kt * P:(kt + 1) * P],
                                           qS[0:K_EXP[L], h, c * CH + off:(c + 1) * CH], start=True, stop=not diagonal)
                    if diagonal:
                        mmi = nc.tensor.matmul(bank[:, off:off + P], identb[:], mask_k[:], start=False, stop=True)
                mmi.then_inc(s_full, 1)

            def times_v(L, s):
                g, c, kt, off, _ = step_span(s)
                cg = STEPS[s][0]
                n = L * N_STEP + s
                pe.wait_ge(s_free, 2 * (n + 1))
                if kt == 0 and L * NC * NG + cg >= 1:
                    pe.wait_ge(o_taken, L * NC * NG + cg)
                bank = ps[:, 7]
                for h in range(G):
                    mmi = nc.tensor.matmul(bank[32 * h:32 * h + 32, off:CH], v1[:, kt, g * G + h, :],
                                           prob[:, n % 3, h, off:CH], start=kt == 0, stop=s == LAST_STEP[cg])
                mmi.then_inc(pv_done, 1)

            def attention(L):
                m_n = L * N_MAX
                pe.wait_ge(b_free, B_AT["on", L, 0])
                side = V_FIRST
                ready = set()
                for n_entry, entry in enumerate(ORDER):
                    if entry[0] == "max":
                        _, cg, item = entry
                        g, c = cg // NC, cg % NC
                        for n in range(N_QK):
                            mt, nc_, _w = qk_job(n)
                            if mt == g * CJ // NG and nc_ <= c and n not in ready:
                                pe.wait_ge(stacked[n], 16 * (L + 1))
                                ready.add(n)
                        if m_n - L * N_MAX >= M_BANKS or L:
                            pe.wait_ge(m_free, m_n - M_BANKS + 1)
                        max_scores(L, m_n, cg, item)
                        m_n += 1
                        if ("exp", 0, 0) in ORDER[n_entry:]:
                            side_job(L, side)
                            side += 1
                    elif entry[0] == "turn":
                        cg = entry[1]
                        pe.wait_ge(m_free, m_n - M_BANKS + 1)
                        pe.wait_ge(mneg_done, L * NC * NG + cg + 1)
                        nc.tensor.transpose(ps[0:2 * G * TPC, 4 + m_n % M_BANKS, 0:P // 2].bitcast(BF16),
                                            mneg[:, cg % 2].rearrange("p s h t -> p (s h t)"), identb[:]).then_inc(m_full, 1)
                        m_n += 1
                    elif entry[0] == "exp":
                        cg, kt = STEPS[entry[1]]
                        if entry[1:] == (0, 0):
                            pe.wait_ge(a_free, A_AT["onT", L, 0])
                        if kt == 0 and entry[2] == 0:
                            pe.wait_ge(m_stacked[cg % 2], 16 * (L * NC * NG // 2 + cg // 2 + 1))
                        exp_scores(L, entry[1], entry[2])
                    else:
                        times_v(L, entry[1])

            def out_projection(L):
                pe.wait_ge(m_free, (L + 1) * N_MAX)
                pe.wait_ge(o_taken, (L + 1) * NC * NG)
                pe.wait_ge(s_free, 2 * (L + 1) * N_STEP)
                for t in range(NT + 2):
                    if t < NT:
                        bank = take_b(("on", L, t))
                        for g in range(NG):
                            mmi = nc.tensor.transpose(bank[:, g * P:(g + 1) * P], oT[:, g, t * P:(t + 1) * P], ident[:])
                        mmi.then_inc(b_full, 1)
                    if 1 <= t <= NT:
                        bank = take_a(("onT", L, t - 1))
                        pe.wait_ge(b_free, B_AT["on", L, t - 1] + 1)
                        for j in range(CJ):
                            mmi = nc.tensor.transpose(bank[:, j * P:(j + 1) * P], xn[:, t - 1, j * P:(j + 1) * P], ident[:])
                        mmi.then_inc(a_full, 1)
                    if t >= 2:
                        bank = take_b(("wo", L, t - 2))
                        pe.wait_ge(a_free, A_AT["onT", L, t - 2] + 1)
                        for j in range(CJ):
                            mmi = nc.tensor.matmul(bank[:, 0:C], onT[:, t % 2, j], attn_w(L, 3)[:, j, :], start=j == 0, stop=j == CJ - 1)
                        mmi.then_inc(b_full, 1)

            def ffn(L):
                ring = (take_a, a_full) if L == 0 else (take_b, b_full)
                ln_transposes("ffnT", 2 * L + 1, 0, L, *ring)
                if L == 1:
                    pe.wait_ge(w8_round, 2)
                for c in range(NC):
                    for ht in range(HT):
                        if (c, ht) == (0, 1):
                            ln_transposes("ffnT", 2 * L + 1, 1, L, *ring)
                        r = hid_rows(L, ht)
                        for m, (name, take, full) in enumerate((("gate", take_a, a_full), ("up", take_b, b_full))):
                            bank = take((name, L, c, ht))
                            if L == 0 and ht == 0:
                                pe.wait_ge(a_free, A_AT["ffnT", L, (c + 1) * TPC - 1] + 1)
                            if L == 1 and ht == 0:
                                pe.wait_ge(b_free, B_AT["ffnT", L, (c + 1) * TPC - 1] + 1)
                            if L == 0:
                                for j in range(CJ):
                                    mmi = nc.tensor.matmul(bank[0:r, :], gu0T[:, m, j, ht * P:ht * P + r],
                                                           xnT[:, j, c * CH:(c + 1) * CH], start=j == 0, stop=j == CJ - 1)
                            else:
                                for j in range(CJ):
                                    for s in range(2):
                                        mmi = nc.tensor.matmul(bank[:, :], gu1[:, m, j, ht * P:(ht + 1) * P],
                                                               xhl[:, j, s, c * CH:(c + 1) * CH],
                                                               start=j + s == 0, stop=j == CJ - 1 and s == 1)
                            mmi.then_inc(full, 1)
                for t in range(NT):
                    bank = take_b(("down", L, t))
                    if L == 0:
                        pe.wait_ge(f_done, (t // TPC + 1) * HT)
                        for ht in range(HT):
                            r = hid_rows(0, ht)
                            mmi = nc.tensor.matmul(bank[:, 0:C], fT[0:r, ht, t * P:(t + 1) * P], d0T[0:r, ht, :],
                                                   start=ht == 0, stop=ht == HT - 1)
                    else:
                        if t == 0:
                            pe.wait_ge(w8_round, 3)
                        for s, done in enumerate((f_hi, f_mid, f_lo)):
                            pe.wait_ge(done, (t // TPC + 1) * HT)
                            for ht in range(HT):
                                mmi = nc.tensor.matmul(bank[:, 0:C], f3[s][:, ht, t * P:(t + 1) * P], d1[:, ht, :],
                                                       start=s + ht == 0, stop=s == 2 and ht == HT - 1)
                    mmi.then_inc(b_full, 1)

            pe.wait_ge(consts, 1)
            for L in range(LAYERS):
                ln_transposes("xnT", 2 * L, 0, L, take_a, a_full)
                if L == 0:
                    pe.wait_ge(w0_in, 16 * 2)
                for n in range(N_QK):
                    if n == QK_FIRST:
                        ln_transposes("xnT", 2 * L, 1, L, take_a, a_full)
                    mt, c, w = qk_job(n)
                    bank = take_b(("qk", L, n))
                    pe.wait_ge(a_free, A_AT["xnT", L, (c + 1) * TPC - 1] + 1)
                    for j in range(CJ):
                        mmi = nc.tensor.matmul(bank[:, :], attn_w(L, w)[:, j, mt * P:(mt + 1) * P],
                                               xnT[:, j, c * CH:(c + 1) * CH], start=j == 0, stop=j == CJ - 1)
                    mmi.then_inc(b_full, 1)
                if L == 0:
                    bank = take_b(("bias",))
                    pe.wait_ge(bvo_in, 16 * 2)
                    pe.wait_ge(wvo_in, 16 * 2)
                    for j in range(CJ):
                        mmi = nc.tensor.matmul(bank[:, 0:C], bv[:, j:j + 1].to_broadcast([P, P]), w0[:, 3, j, :],
                                               start=j == 0, stop=j == CJ - 1)
                    mmi.then_inc(b_full, 1)
                for side in range(V_FIRST):
                    side_job(L, side)
                if L == 0:
                    pe.wait_ge(consts, 2)
                    pe.wait_ge(tail_in, 16)
                else:
                    pe.wait_ge(ones_k, 1)
                attention(L)
                out_projection(L)
                ffn(L)

        @block.scalar
        def _(act):
            for m, n in enumerate(("Wq", "Wk")):
                act.dma_start(w0[:, m], a[f"L0_attn_{n}"].rearrange("(j p) o -> p j o", p=P)).then_inc(w0_in, 16)
            for m, n in enumerate(("bq", "bk")):
                act.dma_start(bqk[:, m], a[f"L0_attn_{n}"].rearrange("(j p) -> p j", p=P)).then_inc(b0_in, 16)

            def bank_a(job):
                n = A_AT[job]
                act.wait_ge(a_full, n + 1)
                return ps[:, n % 4]

            def drain_transposed(job, L, tiles=range(NT)):
                for t in tiles:
                    bank = bank_a((job, L, t))
                    nc.scalar.copy(xnT[:, :, t * P:(t + 1) * P], bank[:, 0:C].rearrange("p (j t) -> p j t", j=CJ)).then_inc(a_free, 1)

            def qk_parts(L):
                for n in range(N_QK + 1):
                    if n < N_QK:
                        mt, _, w = qk_job(n)
                        job = B_AT["qk", L, n]
                        act.wait_ge(b_full, job + 1)
                        if L * N_QK + n >= 4:
                            act.wait_ge(saved[n % 4], 16 * 3 * (2 * L + n // 4))
                        bias = bqk[:, w, mt:mt + 1] if L == 0 else 0.0
                        nc.scalar.activation(parts[:, n % 4, 0], ps[:, 4 + job % 4], ACT.Identity, bias=bias).then_inc(hi_done, 1)
                    if n >= 1:
                        act.wait_ge(b_free, B_AT["qk", L, n - 1] + 1)
                        nc.scalar.copy(parts[:, (n - 1) % 4, 1], rest[:, (n - 1) % 2]).then_inc(mid_done, 1)

            for L in range(LAYERS):
                drain_transposed("xnT", L)
                if L == 0:
                    act.wait_ge(b0_in, 16 * 2)
                qk_parts(L)
                if L == 0:
                    act.wait_ge(consts, 2)
                for t in range(NT):
                    bank = bank_a(("v", L, t))
                    nc.scalar.copy(v1[:, t, :, 0:HD], bank[:, 0:C].rearrange("p (h d) -> p h d", h=NH)).then_inc(a_free, 1)
                if L == 0:
                    for m in range(4):
                        bank = bank_a(("w1T", m))
                        nc.scalar.copy(w1T[:, m].rearrange("p j o -> p (j o)"), bank).then_inc(a_free, 1)
                    for m, name in enumerate(("gateT", "upT")):
                        for k in range(HT // 2):
                            bank = bank_a((name, k))
                            w = hid_rows(0, 2 * k) + hid_rows(0, 2 * k + 1)
                            nc.scalar.copy(gu0T[:, m, :, 2 * k * P:2 * k * P + w],
                                           bank.rearrange("p (j o) -> p j o", j=CJ)[:, :, 0:w]).then_inc(a_free, 1)
                    for k in range(HT // 2):
                        bank = bank_a(("downT", k))
                        r = hid_rows(0, 2 * k + 1)
                        if r == P:
                            nc.scalar.copy(d0T[:, 2 * k:2 * k + 2].rearrange("p k o -> p (k o)"), bank).then_inc(a_free, 1)
                        else:
                            nc.scalar.copy(d0T[:, 2 * k], bank[:, 0:C])
                            nc.scalar.copy(d0T[0:r, 2 * k + 1], bank[0:r, C:2 * C]).then_inc(a_free, 1)
                for s in range(N_STEP):
                    off = step_span(s)[3]
                    n = L * N_STEP + s
                    if n >= 3:
                        act.wait_ge(pv_done, n - 2)
                    for pair in range(G // 2):
                        m = 2 * n + pair
                        act.wait_ge(s_full, m + 1)
                        nc.scalar.activation(prob[:, n % 3, 2 * pair:2 * pair + 2, off:CH],
                                             ps[:, 2 * (m % 2):2 * (m % 2) + 2, off:CH], ACT.Exp, scale=SCALE).then_inc(s_free, 1)
                for t in range(NT):
                    bank = bank_a(("onT", L, t))
                    if t >= 2:
                        act.wait_ge(b_full, B_AT["wo", L, t - 2] + 1)
                    nc.scalar.copy(onT[:, t % 2].rearrange("p j q -> p (j q)"), bank[:, 0:C]).then_inc(a_free, 1)
                def transposed_half(half):
                    tiles = range(TPC * half, TPC * (half + 1))
                    if L == 0:
                        drain_transposed("ffnT", L, tiles)
                        return
                    for t in tiles:
                        job = B_AT["ffnT", L, t]
                        act.wait_ge(b_full, job + 1)
                        nc.scalar.copy(xhl[:, :, 0, t * P:(t + 1) * P],
                                       ps[:, 4 + job % 4, 0:C].rearrange("p (j t) -> p j t", j=CJ)).then_inc(fx_hi, 1)

                def hidden_hi(n):
                    if n >= 0:
                        act.wait_ge(f_done, NC * HT + n + 1)
                        nc.scalar.copy(f3[0][:, n % HT, n // HT * CH:(n // HT + 1) * CH], f_whole[:, n % 3]).then_inc(f_hi, 1)

                def hidden_mid(n):
                    if n >= 0:
                        act.wait_ge(f_left, n + 1)
                        nc.scalar.copy(f3[1][:, n % HT, n // HT * CH:(n // HT + 1) * CH], f_rest[:, n % 3]).then_inc(f_mid, 1)

                transposed_half(0)
                if L == 1:
                    act.wait_ge(ffn1s_in, 16 * 3)
                for c in range(NC):
                    for ht in range(HT):
                        if (c, ht) == (0, 1):
                            transposed_half(1)
                        r = hid_rows(L, ht)
                        n = (L * NC + c) * HT + ht
                        bank = bank_a(("gate", L, c, ht))
                        if n >= 2:
                            act.wait_ge(f_done, n - 1)
                        scale = 1.0 if L == 0 else s1[:, 0, ht:ht + 1]
                        nc.scalar.activation(sg[0:r, n % 2], bank[0:r], ACT.Silu, scale=scale).then_inc(a_free, 1)
                        if L == 1:
                            hidden_hi(c * HT + ht - 1)
                            hidden_mid(c * HT + ht - 2)
                if L == 1:
                    hidden_hi(NC * HT - 1)
                    hidden_mid(NC * HT - 2)
                    hidden_mid(NC * HT - 1)

        @block.vector
        def _(dve):
            k = [0]

            def chain(ins):
                ins.then_inc(dve_step, 1)
                k[0] += 1

            def settle():
                dve.wait_ge(dve_step, k[0])

            def bank_b(job):
                n = B_AT[job]
                dve.wait_ge(b_full, n + 1)
                return ps[:, 4 + n % 4]

            def ln_stats(t):
                chain(nc.vector.bn_stats(stats[:, t], x[:, t]))
                settle()
                ins = nc.vector.bn_aggr(mv[:, t], stats[:, t])
                if t % 4 == 3:
                    ins.then_inc(stats_done, 1)

            def ln_normalise(ln, half):
                dve.wait_ge(rstd_done, 2 * ln + half + 1)
                dve.wait_ge(stats_done, 2 * ln + half + 1)
                for t in range(TPC * half, TPC * (half + 1)):
                    nc.vector.tensor_scalar(xn[:, t], x[:, t], mv[:, t, 0:1], rstd[:, t:t + 1],
                                            ALU.subtract, ALU.mult).then_inc(xn_done, 1)

            def round_w8(n):
                dve.wait_ge(w8_in, 16 * (n + 1))
                if n:
                    dve.wait_ge(w8_round, n)
                nc.vector.tensor_scalar(w8m.bitcast(I32), w8.bitcast(I32), 0x7F800000, None, ALU.bitwise_and).then_inc(w8_exp, 1)

            def add_to_x(job, L, t):
                bank = bank_b((job, L, t))
                ins = nc.vector.tensor_tensor(x[:, t], bank[:, 0:C], x[:, t], ALU.add)
                return ins

            def attention(L):
                m_n = L * N_MAX
                left = {}
                for entry in ORDER:
                    if entry[0] == "max":
                        _, cg, (qt, part, heads, key0, keys) = entry
                        slot = cg % 2
                        dve.wait_ge(m_full, m_n + 1)
                        src = ps[:, 4 + m_n % M_BANKS, 0:len(heads) * keys].rearrange("p (h k) -> p h k", h=len(heads))
                        ins = nc.vector.tensor_reduce(mx[:, slot, qt, heads[0]:heads[-1] + 1, part], src, AX_X, ALU.max)
                        ins.then_inc(m_free, 1)
                        m_n += 1
                        left[cg] = left.get(cg, len(max_items(cg % NC))) - 1
                        if left[cg] == 0:
                            negate_max(L, cg, m_n)
                    elif entry[0] == "turn":
                        n = L * NC * NG + entry[1]
                        dve.wait_ge(m_full, m_n + 1)
                        if n >= 2:
                            dve.wait_ge(m_stacked[n % 2], 16 * (n // 2))
                        nc.vector.tensor_copy(mT[:, entry[1] % 2], ps[0:2 * G * TPC, 4 + m_n % M_BANKS, 0:P // 2].bitcast(BF16)).then_inc(mT_done, 1)
                        dve.wait_ge(mT_done, n + 1)
                        nc.vector.engine_nop().then_inc(m_free, 1)
                        m_n += 1
                    elif entry[0] == "pv" and entry[1] == LAST_STEP[STEPS[entry[1]][0]]:
                        cg = STEPS[entry[1]][0]
                        if L == 1 and cg == 0:
                            dve.wait_ge(w8_round, 3)
                        dve.wait_ge(pv_done, L * N_STEP + entry[1] + 1)
                        g, c = cg // NC, cg % NC
                        nc.vector.tensor_copy(oT[:, g, c * CH:(c + 1) * CH], ps[:, 7]).then_inc(o_taken, 1)

            def negate_max(L, cg, m_n):
                slot = cg % 2
                dve.wait_ge(m_free, m_n)
                both = mx[:, slot].rearrange("p t h s -> p (t h) s")
                if cg % NC:
                    chain(nc.vector.tensor_tensor(mm[:, slot], both[:, :, 0], both[:, :, 1], ALU.max))
                    settle()
                    top = mm[:, slot].rearrange("p (t h) -> p h t", h=G)
                else:
                    top = both[:, :, 1].rearrange("p (t h) -> p h t", h=G)
                chain(nc.vector.tensor_scalar(mneg[:, slot, 0], top, -1.0, None, ALU.mult))
                settle()
                nc.vector.scalar_tensor_tensor(mneg[:, slot, 1], top, -1.0, mneg[:, slot, 0],
                                               ALU.mult, ALU.subtract).then_inc(mneg_done, 1)

            dve.wait_ge(x_in[0], 16)
            for t in range(0, TPC):
                ln_stats(t)
            dve.wait_ge(x_in[1], 16)
            ln_stats(TPC)
            ln_stats(TPC + 1)
            ln_normalise(0, 0)
            for t in range(TPC + 2, NT):
                ln_stats(t)
            for L in range(LAYERS):
                if L == 0:
                    ln_normalise(0, 1)
                    dve.wait_ge(b0_in, 16 * 2)
                for n in range(N_QK + 1):
                    if n < N_QK:
                        mt, _, w = qk_job(n)
                        bank = bank_b(("qk", L, n))
                        dve.wait_ge(hi_done, L * N_QK + n + 1)
                        if L * N_QK + n >= 2:
                            dve.wait_ge(lo_done, L * N_QK + n - 1)
                        bias = bqk[:, w, mt:mt + 1] if L == 0 else 0.0
                        nc.vector.scalar_tensor_tensor(rest[:, n % 2], bank, bias, parts[:, n % 4, 0],
                                                       ALU.add, ALU.subtract).then_inc(b_free, 1)
                    if n >= 1:
                        m = n - 1
                        dve.wait_ge(mid_done, L * N_QK + m + 1)
                        nc.vector.tensor_tensor(parts[:, m % 4, 2], rest[:, m % 2], parts[:, m % 4, 1], ALU.subtract).then_inc(lo_done, 1)
                if L == 0:
                    bank = bank_b(("bias",))
                    dve.wait_ge(bvo_in, 16 * 2)
                    nc.vector.tensor_tensor(bo[:], bank[:, 0:C], bo[:], ALU.add).then_inc(bo_done, 1)
                    dve.wait_ge(bo_done, 1)
                    nc.vector.engine_nop().then_inc(b_free, 1)
                if L == 1:
                    round_w8(2)
                attention(L)
                if L == 0:
                    dve.wait_ge(x_biased, NT)
                for t in range(NT + 2):
                    if t < NT:
                        bank = bank_b(("on", L, t)).rearrange("p (h d) -> p h d", h=NH)
                        chain(nc.vector.reciprocal(rec[:, t % 2].unsqueeze(2), bank[:, :, HD:HD + 1]))
                        settle()
                        nc.vector.tensor_tensor(xn[:, t].rearrange("p (h d) -> p h d", h=NH), bank[:, :, 0:HD],
                                                rec[:, t % 2].unsqueeze(2).to_broadcast([P, NH, HD]), ALU.mult).then_inc(b_free, 1)
                    if t >= 2:
                        add_to_x("wo", L, t - 2).then_inc(b_free, 1)
                        dve.wait_ge(b_free, B_AT["wo", L, t - 2] + 1)
                        ln_stats(t - 2)
                    if t - 2 == FIRST_HALF_AFTER:
                        ln_normalise(2 * L + 1, 0)

                def transposed_half(half):
                    for t in range(TPC * half, TPC * (half + 1)):
                        bank = bank_b(("ffnT", L, t))[:, 0:C].rearrange("p (j t) -> p j t", j=CJ)
                        dve.wait_ge(fx_hi, t + 1)
                        nc.vector.tensor_tensor(xhl[:, :, 1, t * P:(t + 1) * P], bank, xhl[:, :, 0, t * P:(t + 1) * P],
                                                ALU.subtract).then_inc(b_free, 1)

                def hidden_left(n):
                    if n >= 0:
                        dve.wait_ge(f_hi, n + 1)
                        if n >= 3:
                            dve.wait_ge(f_lo, n - 2)
                        nc.vector.tensor_tensor(f_rest[:, n % 3], f_whole[:, n % 3], f3[0][:, n % HT, n // HT * CH:(n // HT + 1) * CH],
                                                ALU.subtract).then_inc(f_left, 1)

                if L == 1:
                    transposed_half(0)
                ln_normalise(2 * L + 1, 1)
                for c in range(NC):
                    for ht in range(HT):
                        if L == 0 and ht == 3:
                            round_w8(c)
                        if L == 1 and (c, ht) == (0, 1):
                            transposed_half(1)
                        r = hid_rows(L, ht)
                        n = (L * NC + c) * HT + ht
                        bank = bank_b(("up", L, c, ht))
                        dve.wait_ge(a_free, A_AT["gate", L, c, ht] + 1)
                        if L == 0:
                            ins = nc.vector.tensor_tensor(fT[0:r, ht, c * CH:(c + 1) * CH], bank[0:r], sg[0:r, n % 2], ALU.mult)
                        else:
                            k1 = n - NC * HT
                            if k1 >= 3:
                                dve.wait_ge(f_hi, k1 - 2)
                                dve.wait_ge(f_left, k1 - 2)
                            ins = nc.vector.scalar_tensor_tensor(f_whole[:, k1 % 3], bank[0:r], s1[:, 1, ht:ht + 1], sg[:, n % 2],
                                                                 ALU.mult, ALU.mult)
                        ins.then_inc(f_done, 1)
                        dve.wait_ge(f_done, n + 1)
                        nc.vector.engine_nop().then_inc(b_free, 1)
                        if L == 1:
                            hidden_left(k1 - 1)
                if L == 1:
                    hidden_left(NC * HT - 1)
                for t in range(NT):
                    if L == 0:
                        add_to_x("down", L, t).then_inc(b_free, 1)
                        dve.wait_ge(b_free, B_AT["down", L, t] + 1)
                        ln_stats(t)
                        if t == FIRST_HALF_AFTER:
                            ln_normalise(2, 0)
                        if t == NT - 1:
                            ln_normalise(2, 1)
                    else:
                        bank = bank_b(("down", L, t))
                        nc.vector.tensor_tensor(y[:, t % 3], bank[:, 0:C], sd1[:], ALU.mult).then_inc(y_done, 1)
                        dve.wait_ge(y_done, t + 1)
                        nc.vector.tensor_tensor(x[:, t], y[:, t % 3], x[:, t], ALU.add).then_inc(x_final, 1)
                        if t < NT - 4:
                            nc.vector.engine_nop().then_inc(b_free, 1)


_INS = ["L0_attn_x", "L0_attn_Wq", "L0_attn_bq", "L0_attn_Wk", "L0_attn_bk", "L0_attn_Wv", "L0_attn_bv", "L0_attn_Wo",
        "L0_attn_bo", "L0_ffn_wq_gate", "L0_ffn_s_gate", "L0_ffn_wq_up", "L0_ffn_s_up", "L0_ffn_wq_down",
        "L0_ffn_s_down", "L1_attn_Wq", "L1_attn_Wk", "L1_attn_Wv", "L1_attn_Wo", "L1_ffn_gate_w", "L1_ffn_up_w",
        "L1_ffn_down_w", "L1_ffn_gate_scale", "L1_ffn_up_scale", "L1_ffn_down_scale"]


def kernel(**inputs):
    import concourse.bacc as bacc
    from concourse.bass_utils import run_bass_kernel_spmd

    nc = bacc.Bacc("TRN2", target_bir_lowering=False, num_devices=1)
    arrays, aps = {}, {}
    for name in _INS:
        arr = np.ascontiguousarray(inputs[name])
        arrays[f"in_{name}"] = arr
        aps[name] = nc.dram_tensor(f"in_{name}", arr.shape, mybir.dt.from_np(arr.dtype), kind="ExternalInput").ap()
    arrays["alibi_tail"] = alibi_tail()
    tail = nc.dram_tensor("alibi_tail", arrays["alibi_tail"].shape, BF16, kind="ExternalInput").ap()
    out = nc.dram_tensor("out", (1, T, C), F32, kind="ExternalOutput").ap()
    two_layer_kernel(nc, aps, out, tail)
    r = run_bass_kernel_spmd(nc, [arrays], core_ids=[0])
    return r.results[0]["out"]
```
